# Optimizing a Trainium2 kernel written in Bass

```python
import numpy as np
import jax
import jax.numpy as jnp

def _softmax(x, axis=-1):
    return jax.nn.softmax(x, axis=axis)

def _gelu(x):
    return jax.nn.gelu(x, approximate=True)

def _silu(x):
    return jax.nn.silu(x)

def _sigmoid(x):
    return jax.nn.sigmoid(x)

def _layernorm(x, axis=-1, eps=1e-05):
    m = jnp.mean(x, axis=axis, keepdims=True)
    v = jnp.var(x, axis=axis, keepdims=True)
    return (x - m) / jnp.sqrt(v + eps)

def _scatter_add(tgt, idx, src, axis=0):
    return tgt.at[idx].add(src)

def _segment_sum(src, seg, n):
    return jax.ops.segment_sum(src, seg, n)
kernel_name = 'mk_decoder_preln_d1_seqx_r8_fd4852'

def setup_inputs(seed: int=0):
    np.random.seed(seed)
    _w = jnp.asarray

    def _rec_inputs():
        import jax
        import jax.numpy as jnp
        _rk = jax.random.key(seed)
        x = -0.000125 + 0.9999 * jax.random.normal(jax.random.fold_in(_rk, 1), (32, 64, 512), jnp.float32)
        _lenS = 64 - jax.random.randint(jax.random.fold_in(_rk, 7), (32,), 0, max(1, 64 // 4) + 1, jnp.int32)
        _lenS2 = 64 - jax.random.randint(jax.random.fold_in(_rk, 8), (32,), 0, max(1, 64 // 4) + 1, jnp.int32)
        _ctx_4096P = jax.random.normal(jax.random.fold_in(_rk, 11), (32, 16, 512), jnp.float32)
        _ctx_4096c = jax.random.dirichlet(jax.random.fold_in(_rk, 511), 0.3 * jnp.ones((16,), jnp.float32), (32, 64))
        _ctx_4096t = jnp.einsum('bsk,bkd->bsd', _ctx_4096c, _ctx_4096P)
        _ctx_4096t = _ctx_4096t * jax.lax.rsqrt(jnp.mean(jnp.square(_ctx_4096t)) + 1e-12) * 0.953939
        ctx_4096 = -1.52775e-05 + 0.999936 * (_ctx_4096t + 0.3 * jax.random.normal(jax.random.fold_in(_rk, 611), (32, 64, 512), jnp.float32))
        return (x, ctx_4096)
    x, ctx_4096 = _rec_inputs()

    def _L0_attn_setup():
        import jax, jax.numpy as jnp
        import numpy as np
        NF4 = jnp.array([-1.0, -0.6961928009986877, -0.5250730514526367, -0.39491748809814453, -0.28444138169288635, -0.18477343022823334, -0.09105003625154495, 0.0, 0.07958029955625534, 0.16093020141124725, 0.24611230194568634, 0.33791524171829224, 0.44070982933044434, 0.5626170039176941, 0.7229568362236023, 1.0], dtype=jnp.float32)
        BLOCK = 64

        def _dequant(codes, scales):
            w = NF4[codes]
            O, I = w.shape
            w = w.reshape(O, I // BLOCK, BLOCK) * scales[:, :, None]
            return w.reshape(O, I)

        def _lin_lora(x, W, A, B):
            base = jnp.einsum('bsh,oh->bso', x, W)
            lora = jnp.einsum('bsr,or->bso', jnp.einsum('bsh,rh->bsr', x, A), B)
            return base + lora
        H, I, R, BT, S = (512, 1792, 16, 2, 256)
        key = jax.random.key(seed)
        ks = jax.random.split(key, 12)
        x = jax.random.normal(ks[0], (BT, S, H), jnp.float32)
        codes_attn = jax.random.randint(ks[1], (4, H, H), 0, 16, jnp.int32)
        scales_attn = jax.random.uniform(ks[2], (4, H, H // BLOCK), jnp.float32) * 0.02
        codes_gu = jax.random.randint(ks[3], (2, I, H), 0, 16, jnp.int32)
        scales_gu = jax.random.uniform(ks[4], (2, I, H // BLOCK), jnp.float32) * 0.02
        codes_down = jax.random.randint(ks[5], (H, I), 0, 16, jnp.int32)
        scales_down = jax.random.uniform(ks[6], (H, I // BLOCK), jnp.float32) * 0.02
        lora_A_h = jax.random.normal(ks[7], (6, R, H), jnp.float32) * 0.02
        lora_A_down = jax.random.normal(ks[8], (R, I), jnp.float32) * 0.02
        lora_B_attn = jax.random.normal(ks[9], (4, H, R), jnp.float32) * 0.02
        lora_B_gu = jax.random.normal(ks[10], (2, I, R), jnp.float32) * 0.02
        lora_B_down = jax.random.normal(ks[11], (H, R), jnp.float32) * 0.02
        return dict(x=x, codes_attn=codes_attn, scales_attn=scales_attn, codes_gu=codes_gu, scales_gu=scales_gu, codes_down=codes_down, scales_down=scales_down, lora_A_h=lora_A_h, lora_A_down=lora_A_down, lora_B_attn=lora_B_attn, lora_B_gu=lora_B_gu, lora_B_down=lora_B_down)
    _L0_attn_all = _L0_attn_setup()
    _L0_attn_in = {k: v for k, v in _L0_attn_all.items() if k in ('codes_attn', 'scales_attn', 'codes_gu', 'scales_gu', 'codes_down', 'scales_down', 'lora_A_h', 'lora_A_down', 'lora_B_attn', 'lora_B_gu', 'lora_B_down')}
    del _L0_attn_all

    def _L0_xattn_setup():
        import jax, jax.numpy as jnp
        import numpy as np
        H = 8
        C = 2

        def _autocorrelation(Q, K, V):
            B, L, D = Q.shape
            d = D // H
            q = Q.reshape(B, L, H, d).transpose(0, 2, 1, 3)
            k = K.reshape(B, L, H, d).transpose(0, 2, 1, 3)
            v = V.reshape(B, L, H, d).transpose(0, 2, 1, 3)
            qf = jnp.fft.fft(q, axis=2)
            kf = jnp.fft.fft(k, axis=2)
            corr = jnp.fft.ifft(qf * jnp.conj(kf), axis=2).real
            topk = int(C * np.log(L))
            w, idx = jax.lax.top_k(corr.transpose(0, 1, 3, 2), topk)
            w = jax.nn.softmax(w, axis=-1)
            pos = jnp.arange(L)[:, None]
            out = jnp.zeros_like(v)
            for i in range(topk):
                g = jnp.minimum(idx[:, :, None, :, i] + pos, L - 1)
                out = out + w[:, :, None, :, i] * jnp.take_along_axis(v, g, axis=2)
            return out.transpose(0, 2, 1, 3).reshape(B, L, D)
        key = jax.random.key(seed)
        k1, k2, k3 = jax.random.split(key, 3)
        B, L, D = (16, 64, 512)
        Q = jax.random.normal(k1, (B, L, D), dtype=jnp.float32)
        K = jax.random.normal(k2, (B, L, D), dtype=jnp.float32)
        V = jax.random.normal(k3, (B, L, D), dtype=jnp.float32)
        return {'Q': Q, 'K': K, 'V': V}
    _L0_xattn_all = _L0_xattn_setup()
    _L0_xattn_in = {k: v for k, v in _L0_xattn_all.items() if k in ()}
    del _L0_xattn_all

    def _L0_ffn_setup():
        import jax, jax.numpy as jnp
        import numpy as np
        R = 16
        LORA_ALPHA = 16
        SCALING = LORA_ALPHA / R
        key = jax.random.key(seed)
        kx, kr, ka = jax.random.split(key, 3)
        B, S, D, DO, E = (4, 256, 512, 512, 8)
        x = jax.random.normal(kx, (B, S, D), dtype=jnp.float32)
        bound_r = 1.0 / np.sqrt(D)
        route_w = jax.random.uniform(kr, (E, D), jnp.float32, -bound_r, bound_r)
        bound_a = 1.0 / np.sqrt(D)
        A = jax.random.uniform(ka, (E, R, D), jnp.float32, -bound_a, bound_a)
        kb = jax.random.fold_in(key, 7)
        Bw = jax.random.normal(kb, (E, DO, R), dtype=jnp.float32) * 0.02
        return {'x': x, 'route_w': route_w, 'A': A, 'Bw': Bw}
    _L0_ffn_all = _L0_ffn_setup()
    _L0_ffn_in = {k: v for k, v in _L0_ffn_all.items() if k in ('route_w', 'A', 'Bw')}
    del _L0_ffn_all
    return {'x': x, 'ctx_4096': ctx_4096, 'L0_attn_codes_attn': _L0_attn_in['codes_attn'], 'L0_attn_scales_attn': _L0_attn_in['scales_attn'], 'L0_attn_codes_gu': _L0_attn_in['codes_gu'], 'L0_attn_scales_gu': _L0_attn_in['scales_gu'], 'L0_attn_codes_down': _L0_attn_in['codes_down'], 'L0_attn_scales_down': _L0_attn_in['scales_down'], 'L0_attn_lora_A_h': _L0_attn_in['lora_A_h'], 'L0_attn_lora_A_down': _L0_attn_in['lora_A_down'], 'L0_attn_lora_B_attn': _L0_attn_in['lora_B_attn'], 'L0_attn_lora_B_gu': _L0_attn_in['lora_B_gu'], 'L0_attn_lora_B_down': _L0_attn_in['lora_B_down'], 'L0_ffn_route_w': _L0_ffn_in['route_w'], 'L0_ffn_A': _L0_ffn_in['A'], 'L0_ffn_Bw': _L0_ffn_in['Bw']}

def reference(x, ctx_4096, L0_attn_codes_attn, L0_attn_scales_attn, L0_attn_codes_gu, L0_attn_scales_gu, L0_attn_codes_down, L0_attn_scales_down, L0_attn_lora_A_h, L0_attn_lora_A_down, L0_attn_lora_B_attn, L0_attn_lora_B_gu, L0_attn_lora_B_down, L0_ffn_route_w, L0_ffn_A, L0_ffn_Bw):
    import jax
    import jax.numpy as jnp

    def _L0_attn_ref(x, codes_attn, scales_attn, codes_gu, scales_gu, codes_down, scales_down, lora_A_h, lora_A_down, lora_B_attn, lora_B_gu, lora_B_down):
        import jax, jax.numpy as jnp
        import numpy as np
        NF4 = jnp.array([-1.0, -0.6961928009986877, -0.5250730514526367, -0.39491748809814453, -0.28444138169288635, -0.18477343022823334, -0.09105003625154495, 0.0, 0.07958029955625534, 0.16093020141124725, 0.24611230194568634, 0.33791524171829224, 0.44070982933044434, 0.5626170039176941, 0.7229568362236023, 1.0], dtype=jnp.float32)
        BLOCK = 64

        def _dequant(codes, scales):
            w = NF4[codes]
            O, I = w.shape
            w = w.reshape(O, I // BLOCK, BLOCK) * scales[:, :, None]
            return w.reshape(O, I)

        def _lin_lora(x, W, A, B):
            base = jnp.einsum('bsh,oh->bso', x, W)
            lora = jnp.einsum('bsr,or->bso', jnp.einsum('bsh,rh->bsr', x, A), B)
            return base + lora
        q = _lin_lora(x, _dequant(codes_attn[0], scales_attn[0]), lora_A_h[0], lora_B_attn[0])
        k = _lin_lora(x, _dequant(codes_attn[1], scales_attn[1]), lora_A_h[1], lora_B_attn[1])
        v = _lin_lora(x, _dequant(codes_attn[2], scales_attn[2]), lora_A_h[2], lora_B_attn[2])
        attn = (q + k + v) / 3.0
        o = _lin_lora(attn, _dequant(codes_attn[3], scales_attn[3]), lora_A_h[3], lora_B_attn[3])
        x1 = x + o
        g = _lin_lora(x1, _dequant(codes_gu[0], scales_gu[0]), lora_A_h[4], lora_B_gu[0])
        u = _lin_lora(x1, _dequant(codes_gu[1], scales_gu[1]), lora_A_h[5], lora_B_gu[1])
        h = jax.nn.silu(g) * u
        d = _lin_lora(h, _dequant(codes_down, scales_down), lora_A_down, lora_B_down)
        return x1 + d

    def _L0_xattn_ref(Q, K, V):
        import jax, jax.numpy as jnp
        import numpy as np
        H = 8
        C = 2

        def _autocorrelation(Q, K, V):
            B, L, D = Q.shape
            d = D // H
            q = Q.reshape(B, L, H, d).transpose(0, 2, 1, 3)
            k = K.reshape(B, L, H, d).transpose(0, 2, 1, 3)
            v = V.reshape(B, L, H, d).transpose(0, 2, 1, 3)
            qf = jnp.fft.fft(q, axis=2)
            kf = jnp.fft.fft(k, axis=2)
            corr = jnp.fft.ifft(qf * jnp.conj(kf), axis=2).real
            topk = int(C * np.log(L))
            w, idx = jax.lax.top_k(corr.transpose(0, 1, 3, 2), topk)
            w = jax.nn.softmax(w, axis=-1)
            pos = jnp.arange(L)[:, None]
            out = jnp.zeros_like(v)
            for i in range(topk):
                g = jnp.minimum(idx[:, :, None, :, i] + pos, L - 1)
                out = out + w[:, :, None, :, i] * jnp.take_along_axis(v, g, axis=2)
            return out.transpose(0, 2, 1, 3).reshape(B, L, D)
        return _autocorrelation(Q, K, V)

    def _L0_ffn_ref(x, route_w, A, Bw):
        import jax, jax.numpy as jnp
        import numpy as np
        R = 16
        LORA_ALPHA = 16
        SCALING = LORA_ALPHA / R
        logits = jnp.einsum('bsd,ed->bse', x, route_w)
        topk_v, topk_idx = jax.lax.top_k(logits, 1)
        E = logits.shape[-1]
        route_weight = jax.nn.one_hot(topk_idx[..., 0], E, dtype=logits.dtype) * topk_v
        h = jnp.einsum('bsd,erd->bser', x, A)
        wh = route_weight[..., None] * h
        out = jnp.einsum('bser,eor->bso', wh, Bw) * SCALING
        return out
    x = x + _L0_attn_ref(_layernorm(x, axis=-1), L0_attn_codes_attn, L0_attn_scales_attn, L0_attn_codes_gu, L0_attn_scales_gu, L0_attn_codes_down, L0_attn_scales_down, L0_attn_lora_A_h, L0_attn_lora_A_down, L0_attn_lora_B_attn, L0_attn_lora_B_gu, L0_attn_lora_B_down)
    x = x + _L0_xattn_ref(_layernorm(x, axis=-1), ctx_4096, ctx_4096)
    x = x + _L0_ffn_ref(_layernorm(x, axis=-1), L0_ffn_route_w, L0_ffn_A, L0_ffn_Bw)
    return x

_drawn_inputs = setup_inputs


def setup_inputs(seed=0):
    import zlib

    import numpy as np

    out = dict(_drawn_inputs(seed))
    spreads = {}
    factors = {'L0_attn_scales_attn': 8.0,
     'L0_attn_scales_gu': 8.0,
     'L0_attn_scales_down': 8.0,
     'L0_attn_lora_A_h': 8.0,
     'L0_attn_lora_A_down': 8.0,
     'L0_attn_lora_B_attn': 8.0,
     'L0_attn_lora_B_gu': 8.0,
     'L0_attn_lora_B_down': 8.0,
     'L0_ffn_route_w': 22.504,
     'ctx_4096': 8.0,
     'L0_ffn_A': 8.0,
     'L0_ffn_Bw': 8.0}
    for name, (base, spread) in spreads.items():
        noise = np.random.default_rng([zlib.crc32(name.encode()), seed]).standard_normal(out[name].shape)
        drawn = base * np.exp(spread * noise) if base else spread * noise
        out[name] = jnp.asarray(drawn.astype(out[name].dtype))
    for name, factor in factors.items():
        out[name] = (out[name] * factor).astype(out[name].dtype)
    return out
```

```python
from contextlib import ExitStack

import concourse.bass as bass
import numpy as np
from concourse import mybir

F32 = mybir.dt.float32
F32R = mybir.dt.float32r
I32 = mybir.dt.int32
ALU = mybir.AluOpType
ACT = mybir.ActivationFunctionType
AX = mybir.AxisListType

P = 128
D = 512
KT = D // P
SEQS, L = 32, 64
T = SEQS * L
TT = T // P
CH = 512
NCH = T // CH
SUB = CH // P
FF = 1792
NFT = FF // P
NG = NFT // 2
QB = 64
R = 16
E = 8
TOPK = int(2 * np.log(L))
assert TOPK == 8 and D == CH
EPS = 1e-5
MARK = -3.0e38

NAT = 3 * KT
ATT = 4 * KT
PER = 6
UNITS = ATT + PER * NG

LINES = [(0.30380717, 1.1266502),
         (0.0851821, -0.009434006),
         (0.13015553, 0.12570463),
         (0.10279457, -0.07326305),
         (0.099667944, 0.0145624615),
         (0.16033982, -0.3994219)]
NL = len(LINES)
SLOPE_LOW = 0.09105003625154495
SLOPE_HIGH = 0.07958029955625534
LAST = (0.5, -3.0)
MIX = 8

SPEC, KRE, KIM, NEG, NRE, NIM, INV_A, INV_B, OUT_A, OUT_B, OUT_NA, OUT_NB = range(12)


def spectral_matrices():
    n = np.arange(L)
    th = 2 * np.pi / L
    re, im, odd = np.arange(L // 2 + 1), np.arange(1, L // 2), np.arange(L // 2) + 0.5
    cos = lambda f: np.cos(th * np.outer(f, n))
    sin = lambda f: np.sin(th * np.outer(f, n))
    two = lambda a, b: np.vstack([a, b])
    spec = two(cos(re), -sin(im))
    kre = two(cos(re), cos(im))
    kre[0, L - 1] += L
    kim = two(-sin(re), -sin(im))
    kim[0], kim[L // 2] = 1, 0
    neg = two(cos(odd), -sin(odd))
    less_last = np.eye(L)
    less_last[:, L - 1] -= 1
    nre = two(cos(odd), cos(odd)) @ less_last
    nim = two(-sin(odd), -sin(odd)) @ less_last
    c = np.full((L // 2 + 1, 1), 2 / L)
    c[0] = c[-1] = 1 / L
    ci = 2 / L
    inv_a = two(c * cos(re), -ci * sin(im))
    inv_a[0] = 0
    inv_b = two(c * sin(re), ci * cos(im))
    inv_b[0] = 1 / L
    out_a = two(c * cos(re), ci * sin(im)) / 2
    out_b = two(-c * sin(re), ci * cos(im)) / 2
    out_b[0] = 0
    out_na = two(cos(odd), sin(odd)) * ci / 2
    out_nb = two(-sin(odd), cos(odd)) * ci / 2
    forward = [m.T for m in (spec, kre, kim, neg, nre, nim)]
    mats = forward + [inv_a, inv_b, out_a, out_b, out_na, out_nb]
    both = np.zeros((P, len(mats), P), np.float32)
    for k, m in enumerate(mats):
        both[:L, k, :L] = m
        both[L:, k, L:] = m
    return both



def build(nc, x, ctx_in, codes, scale_nat, scale_rows, lora_attn, lora_h, lora_ft, lora_down_b,
          router, expert_b, spectral, eye_in, out):
    st = ExitStack()
    sem = lambda name: st.enter_context(nc.semaphore(name))

    place = {"at": nc.sbuf_base}

    def sb(name, shape, dt=F32, at=None):
        if at is not None:
            place["at"] = at
        start = -(-place["at"] // 32) * 32
        place["at"] = start + 4 * int(np.prod(shape[1:]))
        return nc.alloc_sbuf_tensor_at(name, shape, dt, offset=start)

    acc = sb("acc", [P, TT, D])
    eye = sb("eye", [P, P])
    stats = sb("stats", [P, SUB, 6])
    mv = sb("mv", [P, SUB, 2])
    ve = sb("ve", [P, SUB])
    pw = sb("pw", [P, SUB])
    nt = sb("nt", [P, 2, SUB])
    rstd = sb("rstd", [P, NCH, SUB])
    nmr = sb("nmr", [P, NCH, SUB])
    half = sb("half", [P, SUB])
    dq_at = place["at"]
    codes_sb = sb("codes_sb", [P, 2, CH], I32)
    scale_sb = sb("scale_sb", [P, 2, CH])
    xc = sb("xc", [P, 2, CH])
    line = sb("line", [P, NL, CH])
    last_line = sb("last_line", [P, CH])
    wt = sb("wt", [P, 2, CH])
    ldown = sb("ldown", [P, D])
    lh = sb("lh", [P, 2, D])
    lft = sb("lft", [P, 2, 3 * P])
    nat_scale = sb("nat_scale", [P, NAT, D // QB])
    x_hi = sb("x_hi", [P, KT, T], F32R)
    x_lo = sb("x_lo", [P, KT, T], F32R)
    w0_at = place["at"]
    w_hi = [sb("w_hi0", [P, PER, CH], F32R)]
    w_lo = [sb("w_lo0", [P, PER, CH], F32R)]
    w1_at = place["at"]
    w_hi.append(sb("w_hi1", [P, PER, CH], F32R))
    w_lo.append(sb("w_lo1", [P, PER, CH], F32R))
    h_at = place["at"]
    h_hi = sb("h_hi", [P, 2, 2, CH], F32R)
    h_lo = sb("h_lo", [P, 2, 2, CH], F32R)
    hf = sb("hf", [P, 2, CH])
    end_b = place["at"]
    wsum = sb("wsum", [P, KT, D], at=w1_at)
    w3 = sb("w3", [P, KT, D])
    lattn = sb("lattn", [P, 4, D])
    x1f = sb("x1f", [P, 2, CH], at=w1_at)
    mt_hi = sb("mt_hi", [P, KT, D], F32R, at=h_at)
    mt_lo = sb("mt_lo", [P, KT, D], F32R)
    xhat = sb("xhat", [P, 2, D])
    spec = sb("spec", [P, 12, P], at=dq_at)
    rt = sb("rt", [P, KT, P + E])
    eb = sb("eb", [P, D])
    prio = sb("prio", [P, E])
    ctx = sb("ctx", [P, 2, D])
    assert place["at"] <= dq_at + 4 * (2 * 3 + NL + 1 + 2) * CH
    two = lambda name, shape=(D,), at=None: sb(name, [P, 2, *shape], at=at)
    xq = two("xq", at=dq_at + 40960)
    qs = two("qs")
    kre, kim, nre, nim = two("kre"), two("kim"), two("nre"), two("nim")
    p1, p2 = two("p1"), two("p2")
    top = two("top", (8, TOPK))
    topd = two("topd", (8, TOPK))
    zs, rz = two("zs", (8,)), two("rz", (8,))
    cd = two("cd")
    ex, en = two("ex"), two("en")
    mark = two("mark")
    wl = two("wl")
    wts = two("wts")
    wns = two("wns")
    pc1, pc2, pn1, pn2 = two("pc1"), two("pc2"), two("pn1"), two("pn2")
    x3 = two("x3")
    xh3 = two("xh3")
    x3t = two("x3t")
    mx, sc, m2, rw = two("mx", (8,)), two("sc", (E,)), two("m2", (8,)), two("rw", (E,))
    wh, wht = two("wh", (P,)), two("wht", (P,))
    fin = two("fin")
    lst = {k: (sb(f"st{k}", [P, 2, 6]), sb(f"mv{k}", [P, 2, 2]), sb(f"ve{k}", [P, 2]),
               sb(f"pw{k}", [P, 2]), sb(f"na{k}", [P, 2]), sb(f"nb{k}", [P, 2]),
               sb(f"rs{k}", [P, 2])) for k in (2, 3)}
    assert max(end_b, place["at"]) <= nc.sbuf_usable_end
    ps = st.enter_context(nc.psum_tensor("ps", [P, 8, CH], F32))
    FWD0, FWD1, CORR, LAGS, WCYC, WNEG, MISC, ROUTE = range(8)

    started = sem("started")
    zeroed = sem("zeroed")
    eye_in_s, lora_in, nat_in = sem("eye_in"), sem("lora_in"), sem("nat_in")
    x_in = [sem(f"x_in{k}") for k in range(NCH)]
    codes_in = [sem(f"codes_in{k}") for k in range(2)]
    scales_in = [sem(f"scales_in{k}") for k in range(2)]
    lft_in = [sem(f"lft_in{k}") for k in range(2)]
    centred, lined, last_lined = sem("centred"), sem("lined"), sem("last_lined")
    mixed, scaled, folded = sem("mixed"), sem("scaled"), sem("folded")
    hi_done, lo_done, lora_ready = sem("hi_done"), sem("lo_done"), sem("lora_ready")
    al_ready, al_copied = sem("al_ready"), sem("al_copied")
    ln1, pow1 = sem("ln1"), sem("pow1")
    normed, turned, xhi_done, xlo_done = sem("normed"), sem("turned"), sem("xhi"), sem("xlo")
    mt_ready, mt_scaled, mt_hi_done, mt_lo_done = (sem("mt_ready"), sem("mt_scaled"),
                                                   sem("mt_hi_done"), sem("mt_lo_done"))
    x1_ready, x1_copied, x1_hi, x1_lo = sem("x1_ready"), sem("x1_copied"), sem("x1_hi"), sem("x1_lo")
    x1_turned, x1_added = sem("x1_turned"), sem("x1_added")
    gu, silu_done, hmul_done = sem("gu"), sem("silu_done"), sem("hmul_done")
    hhi_done, hlo_done, down, added = sem("hhi_done"), sem("hlo_done"), sem("down"), sem("added")

    def real(n):
        return not isinstance(n, int) or n > 0

    def by_themselves(e, *counts):
        for n in counts:
            if real(n):
                e.compute_val(n)
        e.wait_ge(started, 1)

    def sp_unit(sp, m, b, rows=True):
        u = 2 * m + b
        if real(u - 1):
            sp.wait_ge(centred, u - 1)
        sp.dma_start(codes_sb[:, b, :], row_of(codes, u)).then_inc(codes_in[b], 16)
        if rows:
            sp.wait_ge(scaled, u - 1)
            for h in range(2):
                row = row_of(scale_rows, 2 * u + (h - 2 * NAT))
                sp.dma_start(scale_sb[QB * h:QB * h + QB, b, :],
                             row.to_broadcast([QB, CH])).then_inc(scales_in[b], 16)

    def row_of(dram, n):
        return dram[n] if isinstance(n, int) else dram[bass.ds(n, 1)].rearrange("o p f -> (o p) f")

    def lft_load(sp, f, b):
        sp.wait_ge(lora_ready, 3 * (f - 1))
        sp.dma_start(lft[0:R, b, :], row_of(lora_ft, f)).then_inc(lft_in[b], 16)

    def pool_centre(pool, m, b):
        u = 2 * m + b
        by_themselves(pool, 16 * m + 16, NL * (u - 1), MIX * (u - 2) + 2)
        pool.wait_ge(codes_in[b], 16 * m + 16)
        if real(NL * (u - 1)):
            pool.wait_ge(lined, NL * (u - 1))
        if real(MIX * (u - 2) + 2):
            pool.wait_ge(mixed, MIX * (u - 2) + 2)
        nc.gpsimd.tensor_scalar(xc[:, b], codes_sb[:, b], -7.0, 1.0, ALU.add,
                                ALU.mult).then_inc(centred, 1)
        by_themselves(pool, u + 1, MIX * u)
        pool.wait_ge(centred, u + 1)
        if real(MIX * u):
            pool.wait_ge(mixed, MIX * u)
        nc.gpsimd.tensor_scalar(last_line[:], xc[:, b], LAST[0], LAST[1], ALU.mult,
                                ALU.add).then_inc(last_lined, 1)

    FREE_AFTER = [3, 4, 5, 6, 8, 7]

    def act_lines(act, m, b):
        u = 2 * m + b
        act.wait_ge(centred, u + 1)
        for k, (s, c) in enumerate(LINES):
            if real(MIX * (u - 1) + FREE_AFTER[k]):
                act.wait_ge(mixed, MIX * (u - 1) + FREE_AFTER[k])
            nc.scalar.activation(line[:, k], xc[:, b], ACT.Identity, bias=c,
                                 scale=s).then_inc(lined, 1)

    def dve_mix(dve, m, b):
        u = 2 * m + b
        n, k = MIX * u, NL * u
        X = xc[:, b]
        dve.wait_ge(centred, u + 1)
        dve.wait_ge(lined, k + 1)
        nc.vector.scalar_tensor_tensor(out=line[:, 0], in0=X, scalar=SLOPE_LOW, in1=line[:, 0],
                                       op0=ALU.mult, op1=ALU.min).then_inc(mixed, 1)
        dve.wait_ge(lined, k + 2)
        nc.vector.scalar_tensor_tensor(out=line[:, 1], in0=X, scalar=SLOPE_HIGH, in1=line[:, 1],
                                       op0=ALU.mult, op1=ALU.max).then_inc(mixed, 1)
        for at, frm, op, seen, lines in ((2, 0, ALU.min, 1, 3), (3, 1, ALU.max, 2, 4),
                                         (4, 2, ALU.min, 3, 5), (4, 3, ALU.min, 5, 5),
                                         (4, 5, ALU.max, 6, 6)):
            dve.wait_ge(lined, k + lines)
            dve.wait_ge(mixed, n + seen)
            nc.vector.tensor_tensor(line[:, at], line[:, at], line[:, frm], op).then_inc(mixed, 1)
        dve.wait_ge(last_lined, u + 1)
        dve.wait_ge(mixed, n + 7)
        if real(u - 1):
            dve.wait_ge(folded, u - 1)
        if real(u - 1 - ATT if isinstance(u, int) else u - (1 + ATT)):
            dve.wait_ge(lo_done, u - 1 - ATT if isinstance(u, int) else u - (1 + ATT))
        nc.vector.tensor_tensor(wt[:, b], line[:, 4], last_line[:], ALU.max).then_inc(mixed, 1)

    def pool_scale(pool, m, b, nat=None):
        u = 2 * m + b
        pool.wait_ge(mixed, MIX * u + MIX)
        if nat is not None:
            pool.wait_ge(nat_in, 16)
            s = nat_scale[:, nat, :].unsqueeze(2).to_broadcast([P, D // QB, QB])
            w = wt[:, b].rearrange("p (a q) -> p a q", q=QB)
        else:
            pool.wait_ge(scales_in[b], 32 * (m - NAT // 2) + 32)
            s, w = scale_sb[:, b], wt[:, b]
        nc.gpsimd.tensor_tensor(w, w, s, ALU.mult).then_inc(scaled, 1)

    def pe_lora(pe, m, b, g, k):
        u = 2 * m + b
        ft_b = k // 3
        pe.wait_ge(folded, u - 1)
        if k % 3 == 0:
            pe.wait_ge(lft_in[ft_b], 16 * g + 16)
        if k % 3 < 2:
            for kt in range(KT):
                mm = nc.tensor.matmul(ps[:, 6 + b, kt * P:(kt + 1) * P],
                                      lh[:, k % 3, kt * P:(kt + 1) * P],
                                      lft[:, ft_b, (k % 3) * P:(k % 3 + 1) * P], start=True, stop=True)
        else:
            mm = nc.tensor.matmul(ps[:, 6 + b, :], lft[:, ft_b, 2 * P:3 * P], ldown[:],
                                  start=True, stop=True)
        mm.then_inc(lora_ready, 1)

    def dve_fold(dve, m, b, a=None):
        u = 2 * m + b
        dve.wait_ge(scaled, u + 1)
        if a is not None:
            dst = wsum[:, a % KT] if a < NAT else w3[:, a % KT]
            dve.wait_ge(al_copied, a % KT + 1 if a < NAT else KT + a % KT + 1)
            if KT <= a < NAT:
                dve.wait_ge(folded, u - 3)
            nc.vector.tensor_tensor(dst, dst, wt[:, b], ALU.add).then_inc(folded, 1)
        else:
            dve.wait_ge(lora_ready, u - (ATT - 1))
            nc.vector.tensor_tensor(wt[:, b], wt[:, b], ps[:, 6 + b, :], ALU.add).then_inc(folded, 1)

    def act_hi(act, m, b, gp, g, k):
        u = 2 * m + b
        act.wait_ge(folded, u + 1)
        if k == 0 and not (isinstance(g, int) and g == 0):
            act.wait_ge(x1_turned, KT * NCH)
            if real(4 * NCH * (g - 1)):
                act.wait_ge(down, 4 * NCH * (g - 1))
        nc.scalar.copy(w_hi[gp][:, k], wt[:, b]).then_inc(hi_done, 1)

    def pool_lo(pool, m, b, gp, k):
        u = 2 * m + b
        pool.wait_ge(hi_done, u - (ATT - 1))
        nc.gpsimd.tensor_tensor(w_lo[gp][:, k], wt[:, b], w_hi[gp][:, k].bitcast(F32),
                                ALU.subtract).then_inc(lo_done, 1)

    def x_stats(dve, c):
        n = LNS * c
        dve.wait_ge(x_in[c], 16)
        for s in range(SUB):
            nc.vector.bn_stats(stats[:, s], acc[:, SUB * c + s]).then_inc(ln1, 1)
        if real(n):
            dve.wait_ge(ln1, n)
        for s in range(SUB):
            dve.wait_ge(ln1, n + s + 1)
            nc.vector.bn_aggr(mv[:, s], stats[:, s]).then_inc(ln1, 1)
        dve.wait_ge(ln1, n + 2 * SUB)
        if real(c):
            dve.wait_ge(pow1, c)
        nc.vector.tensor_scalar(ve[:], mv[:, :, 1], EPS, None, ALU.add).then_inc(ln1, 1)

    LNS = 2 * SUB + 5

    def x_pow(pool, c):
        pool.wait_ge(ln1, LNS * c + 2 * SUB + 1)
        nc.gpsimd.tensor_tensor(pw[:], ve[:], half[:], ALU.pow).then_inc(pow1, 1)

    def newton(dve, count, n, v, y, t1, t2, r):
        nc.vector.tensor_tensor(t1, y, y, ALU.mult).then_inc(count, 1)
        dve.wait_ge(count, n + 1)
        nc.vector.scalar_tensor_tensor(out=t2, in0=t1, scalar=-0.5, in1=v, op0=ALU.mult,
                                       op1=ALU.mult).then_inc(count, 1)
        dve.wait_ge(count, n + 2)
        nc.vector.scalar_tensor_tensor(out=r, in0=t2, scalar=1.5, in1=y, op0=ALU.add,
                                       op1=ALU.mult).then_inc(count, 1)

    def x_rstd(dve, c):
        n = LNS * c + 2 * SUB + 1
        dve.wait_ge(pow1, c + 1)
        newton(dve, ln1, n, ve[:], pw[:], nt[:, 0], nt[:, 1], rstd[:, c])
        dve.wait_ge(ln1, n + 3)
        nc.vector.scalar_tensor_tensor(out=nmr[:, c], in0=mv[:, :, 0], scalar=-1.0, in1=rstd[:, c],
                                       op0=ALU.mult, op1=ALU.mult).then_inc(ln1, 1)

    def x_normalise(act, t):
        c, s = divmod(t, SUB)
        act.wait_ge(ln1, LNS * (c + 1))
        if real(t - 1):
            act.wait_ge(turned, t - 1)
        nc.scalar.activation(xhat[:, t % 2], acc[:, t], ACT.Identity, bias=nmr[:, c, s:s + 1],
                             scale=rstd[:, c, s:s + 1]).then_inc(normed, 1)

    def x_turn(pe, t):
        pe.wait_ge(eye_in_s, 16)
        pe.wait_ge(normed, t + 1)
        if real(t - 1):
            pe.wait_ge(xlo_done, t - 1)
        for kt in range(KT):
            mm = nc.tensor.transpose(ps[:, 4 + t % 2, kt * P:(kt + 1) * P],
                                     xhat[:, t % 2, kt * P:(kt + 1) * P], eye[:])
        mm.then_inc(turned, 1)

    def by_tile(xt, t):
        return xt[:, :, t * P:(t + 1) * P]

    def bank_tile(t):
        return ps[:, 4 + t % 2].rearrange("p (k n) -> p k n", k=KT)

    def x_hi_copy(act, t):
        act.wait_ge(turned, t + 1)
        nc.scalar.copy(by_tile(x_hi, t), bank_tile(t)).then_inc(xhi_done, 1)

    def x_lo_sub(dve, t):
        dve.wait_ge(xhi_done, t + 1)
        nc.vector.tensor_tensor(by_tile(x_lo, t), bank_tile(t), by_tile(x_hi, t).bitcast(F32),
                                ALU.subtract).then_inc(xlo_done, 1)

    def pe_mt(pe):
        pe.wait_ge(folded, ATT)
        for kt in range(KT):
            pe.wait_ge(al_copied, 2 * KT)
            for o in range(KT):
                mm = nc.tensor.matmul(ps[:, kt, :], wsum[:, o, kt * P:(kt + 1) * P], w3[:, o],
                                      start=(o == 0), stop=(o == KT - 1))
            mm.then_inc(mt_ready, 1)

    def dve_mt(dve):
        dve.wait_ge(mt_ready, KT)
        for kt in range(KT):
            if real(kt - 1):
                dve.wait_ge(mt_lo_done, kt - 1)
            nc.vector.tensor_scalar(x1f[:, kt % 2], ps[:, kt], 1.0 / 3.0, None,
                                    ALU.mult).then_inc(mt_scaled, 1)
            dve.wait_ge(mt_scaled, 2 * kt + 1)
            diagonal = x1f[:, kt % 2, kt * P:(kt + 1) * P]
            nc.vector.tensor_tensor(diagonal, diagonal, eye[:], ALU.add).then_inc(mt_scaled, 1)

    def act_mt(act):
        for kt in range(KT):
            act.wait_ge(mt_scaled, 2 * kt + 2)
            nc.scalar.copy(mt_hi[:, kt], x1f[:, kt % 2]).then_inc(mt_hi_done, 1)

    def pool_mt(pool):
        for kt in range(KT):
            pool.wait_ge(mt_hi_done, kt + 1)
            nc.gpsimd.tensor_tensor(mt_lo[:, kt], x1f[:, kt % 2], mt_hi[:, kt].bitcast(F32),
                                    ALU.subtract).then_inc(mt_lo_done, 1)

    def three(pe, bank, hi, lo, rhs_hi, rhs_lo, start, stop):
        nc.tensor.matmul(bank, hi, rhs_hi, start=start, stop=False)
        nc.tensor.matmul(bank, hi, rhs_lo, start=False, stop=False)
        return nc.tensor.matmul(bank, lo, rhs_hi, start=False, stop=stop)

    def pe_x1(pe, c):
        chunk = slice(c * CH, (c + 1) * CH)
        pe.wait_ge(mt_lo_done, KT)
        pe.wait_ge(xlo_done, SUB * (c + 1))
        for f in range(KT):
            n = KT * (c - 1) + f + 1
            if real(n):
                pe.wait_ge(x1_hi, n)
            if real(n):
                pe.wait_ge(x1_lo, n)
            for kt in range(KT):
                col = slice(f * P, (f + 1) * P)
                mm = three(pe, ps[:, f, :], mt_hi[:, kt, col], mt_lo[:, kt, col],
                           x_hi[:, kt, chunk], x_lo[:, kt, chunk], kt == 0, kt == KT - 1)
            mm.then_inc(x1_ready, 1)

    def pe_x1_turn(pe, c):
        for f in range(KT):
            n = KT * c + f
            pe.wait_ge(x1_copied, n + 1)
            pe.wait_ge(xlo_done, TT)
            if real(n - 1):
                pe.wait_ge(x1_added, n - 1)
            for s in range(SUB):
                mm = nc.tensor.transpose(ps[:, 4 + f % 2, s * P:(s + 1) * P],
                                         x1f[:, f % 2, s * P:(s + 1) * P], eye[:])
            mm.then_inc(x1_turned, 1)

    def act_x1(act, c):
        chunk = slice(c * CH, (c + 1) * CH)
        for f in range(KT):
            n = KT * c + f
            act.wait_ge(x1_ready, n + 1)
            act.wait_ge(mt_lo_done, KT)
            if real(n - 1):
                act.wait_ge(x1_turned, n - 1)
            nc.scalar.copy(x1f[:, f % 2], ps[:, f]).then_inc(x1_copied, 1)
            act.wait_ge(x1_ready, KT * (c + 1))
            nc.scalar.copy(x_hi[:, f, chunk], ps[:, f]).then_inc(x1_hi, 1)

    def dve_x1(dve, c):
        chunk = slice(c * CH, (c + 1) * CH)
        for f in range(KT):
            n = KT * c + f
            dve.wait_ge(x1_hi, n + 1)
            nc.vector.tensor_tensor(x_lo[:, f, chunk], ps[:, f], x_hi[:, f, chunk].bitcast(F32),
                                    ALU.subtract).then_inc(x1_lo, 1)
            dve.wait_ge(x1_turned, n + 1)
            part = acc[:, SUB * c:SUB * (c + 1), f * P:(f + 1) * P]
            nc.vector.tensor_tensor(part, part, ps[:, 4 + f % 2].rearrange("p (s n) -> p s n", s=SUB),
                                    ALU.add).then_inc(x1_added, 1)

    def pe_gate_up(pe, g, gp, c, tiles=(0, 1)):
        S = 4 * g + c
        chunk = slice(c * CH, (c + 1) * CH)
        for i in tiles:
            for w in range(2):
                if real(2 * S + (i - 1)):
                    pe.wait_ge(silu_done if w == 0 else hmul_done, 2 * S + (i - 1))
                if c == 0:
                    pe.wait_ge(lo_done, PER * g + (3 * i + w + 1))
                if isinstance(g, int) and g == 0:
                    pe.wait_ge(x1_lo, KT * (c + 1))
                    pe.wait_ge(x1_lo, KT * NCH)
                for kt in range(KT):
                    col = slice(kt * P, (kt + 1) * P)
                    mm = three(pe, ps[:, 2 * i + w, :], w_hi[gp][:, 3 * i + w, col],
                               w_lo[gp][:, 3 * i + w, col], x_hi[:, kt, chunk],
                               x_lo[:, kt, chunk], kt == 0, kt == KT - 1)
                mm.then_inc(gu, 1)

    def pe_down(pe, g, gp, c):
        S = 4 * g + c
        pe.wait_ge(hlo_done, 2 * S + 2)
        if c == 0:
            pe.wait_ge(lo_done, PER * g + PER)
        for s in range(SUB):
            if real(4 * S + (s - 1)):
                pe.wait_ge(added, 4 * S + (s - 1))
            if isinstance(S, int) and S == 0:
                pe.wait_ge(x1_added, KT * NCH)
            tok = slice(s * P, (s + 1) * P)
            for i in range(2):
                mm = three(pe, ps[:, 4 + s % 2, :], h_hi[:, c % 2, i, tok], h_lo[:, c % 2, i, tok],
                           w_hi[gp][:, 3 * i + 2], w_lo[gp][:, 3 * i + 2], i == 0, i == 1)
            mm.then_inc(down, 1)

    def act_silu(act, g, c, i):
        S = 4 * g + c
        act.wait_ge(gu, 4 * S + (2 * i + 1))
        if real(2 * S + (i - 1)):
            act.wait_ge(hlo_done, 2 * S + (i - 1))
        nc.scalar.activation(hf[:, i], ps[:, 2 * i], ACT.Silu).then_inc(silu_done, 1)

    def dve_hmul(dve, g, c, i):
        S = 4 * g + c
        dve.wait_ge(silu_done, 2 * S + (i + 1))
        dve.wait_ge(gu, 4 * S + (2 * i + 2))
        nc.vector.tensor_tensor(hf[:, i], hf[:, i], ps[:, 2 * i + 1], ALU.mult).then_inc(hmul_done, 1)

    def act_hhi(act, g, c, i):
        S = 4 * g + c
        act.wait_ge(hmul_done, 2 * S + (i + 1))
        if real(4 * (S - 1)):
            act.wait_ge(down, 4 * (S - 1))
        nc.scalar.copy(h_hi[:, c % 2, i], hf[:, i]).then_inc(hhi_done, 1)

    def pool_hlo(pool, g, c, i):
        S = 4 * g + c
        pool.wait_ge(hhi_done, 2 * S + (i + 1))
        nc.gpsimd.tensor_tensor(h_lo[:, c % 2, i], hf[:, i], h_hi[:, c % 2, i].bitcast(F32),
                                ALU.subtract).then_inc(hlo_done, 1)

    def dve_add(dve, g, c):
        S = 4 * g + c
        for s in range(SUB):
            dve.wait_ge(down, 4 * S + (s + 1))
            if real(4 * S + (s - SUB + 1)):
                dve.wait_ge(added, 4 * S + (s - SUB + 1))
            tile = acc[:, SUB * c + s]
            nc.vector.tensor_tensor(tile, tile, ps[:, 4 + s % 2], ALU.add).then_inc(added, 1)

    SLOTS = [(0, 1), (2,), (3, 4), (5,)]

    def pairs(e, body):
        u0 = lambda g: (ATT + PER) // 2 + PER // 2 * g
        body(0, 0, u0(0), True)
        with e.Fori(0, 2) as it:
            body(it * 2 + 1, 1, it * PER + u0(1), True)
            body(it * 2 + 2, 0, it * PER + u0(2), True)
        body(NG - 2, 1, u0(NG - 2), True)
        body(NG - 1, 0, u0(NG - 1), False)

    def unit(m, k):
        return m + k // 2, k % 2

    def place_of(g, gp, k):
        return (g, gp, k) if k >= 0 else (g - 1, 1 - gp, k + PER)

    const_in, prio_set = sem("const_in"), sem("prio_set")
    ctx_in_s = [sem(f"ctx_in{k}") for k in range(2)]
    out_s = [sem(f"out{k}") for k in range(2)]
    ln = {2: sem("ln2"), 3: sem("ln3")}
    powed = {2: sem("pow2"), 3: sem("pow3")}
    xq_done, xh3_done = sem("xq_done"), sem("xh3_done")
    fwd, evac = sem("fwd"), sem("evac")
    prod, corr_ready = sem("prod"), sem("corr_ready")
    top_done, less_done, topd_done = sem("top_done"), sem("less_done"), sem("topd_done")
    marked, exp_done, summed, divided = sem("marked"), sem("exp_done"), sem("summed"), sem("divided")
    weighed, lag_turned, lag_copied = sem("weighed"), sem("lag_turned"), sem("lag_copied")
    wspec, wneg_copied = sem("wspec"), sem("wneg_copied")
    pcyc, pneg, gathered, x3_done = sem("pcyc"), sem("pneg"), sem("gathered"), sem("x3_done")
    h_turned, h_copied, routed_in = sem("h_turned"), sem("h_copied"), sem("routed_in")
    route, wh_done = sem("route"), sem("wh_done")
    wh_turned, wh_copied, expert, fin_done = (sem("wh_turned"), sem("wh_copied"), sem("expert"),
                                              sem("fin_done"))
    SMALL = 6
    tile_of = lambda big, t: (big[:, t] if isinstance(t, int) else
                              big[:, bass.ds(t, 1)].rearrange("p o d -> p (o d)"))

    def dve_stats(dve, k, src, t, b):
        st_, mv_, ve_ = lst[k][:3]
        n = SMALL * t
        if k == 2:
            by_themselves(dve, t - 1)
            if real(t - 1):
                dve.wait_ge(xq_done, t - 1)
        else:
            by_themselves(dve, t + 1, t - 1)
            dve.wait_ge(x3_done, t + 1)
            if real(t - 1):
                dve.wait_ge(xh3_done, t - 1)
        nc.vector.bn_stats(st_[:, b], src).then_inc(ln[k], 1)
        by_themselves(dve, n + 1)
        dve.wait_ge(ln[k], n + 1)
        nc.vector.bn_aggr(mv_[:, b], st_[:, b]).then_inc(ln[k], 1)
        dve.wait_ge(ln[k], n + 2)
        nc.vector.tensor_scalar(ve_[:, b:b + 1], mv_[:, b, 1:2], EPS, None, ALU.add).then_inc(ln[k], 1)

    def pool_pow(pool, k, t, b):
        pool.wait_ge(ln[k], SMALL * t + 3)
        nc.gpsimd.tensor_tensor(lst[k][3][:, b:b + 1], lst[k][2][:, b:b + 1], half[:, 0:1],
                                ALU.pow).then_inc(powed[k], 1)

    def dve_normalise(dve, k, src, dst, t, b):
        _, mv_, ve_, pw_, na_, nb_, rs_ = lst[k]
        col = slice(b, b + 1)
        n = SMALL * t
        dve.wait_ge(powed[k], t + 1)
        newton(dve, ln[k], n + 3, ve_[:, col], pw_[:, col], na_[:, col], nb_[:, col], rs_[:, col])
        dve.wait_ge(ln[k], n + 6)
        if real(5 * (t - 1) if k == 2 else t - 1):
            dve.wait_ge(fwd if k == 2 else h_turned, 5 * (t - 1) if k == 2 else t - 1)
        nc.vector.tensor_scalar(dst, src, mv_[:, b, 0:1], rs_[:, col], ALU.subtract,
                                ALU.mult).then_inc(xq_done if k == 2 else xh3_done, 1)

    def sp_ctx(sp, t, b):
        if real(5 * (t - 1)):
            sp.wait_ge(fwd, 5 * (t - 1))
        sp.dma_start(ctx[:, b], row_of(ctx_in, t)).then_inc(ctx_in_s[b], 16)

    FWD = [SPEC, KRE, KIM, NRE, NIM]

    def pe_forward(pe, t, b, h):
        n = 5 * t
        for k, mat in enumerate(FWD):
            if k == 0:
                pe.wait_ge(const_in, 48)
                pe.wait_ge(xq_done, t + 1)
            if k == 1:
                pe.wait_ge(ctx_in_s[b], 16 * h + 16)
            if real(n + (k - 1)):
                pe.wait_ge(evac, n + (k - 1))
            if isinstance(t, int) and t == 0:
                pe.wait_ge(added, 4 * NCH * NG)
            nc.tensor.matmul(ps[:, bank_of(b, k)], spec[:, mat], (xq if k == 0 else ctx)[:, b],
                             start=True, stop=True).then_inc(fwd, 1)

    def bank_of(b, k):
        return (b * 5 + k) % 2

    def act_evac(act, t, b):
        n = 5 * t
        for k, dst in enumerate((qs, kre, kim, nre, nim)):
            act.wait_ge(fwd, n + (k + 1))
            if k == 0:
                if real(2 * (t - 1)):
                    act.wait_ge(prod, 2 * (t - 1))
                if real(2 * (t - 1)):
                    act.wait_ge(pcyc, 2 * (t - 1))
                if real(2 * (t - 1)):
                    act.wait_ge(pneg, 2 * (t - 1))
            nc.scalar.copy(dst[:, b], ps[:, bank_of(b, k)]).then_inc(evac, 1)

    def dve_products(dve, t, b):
        for k, (ctx_part, dst) in enumerate(((kre, p1), (kim, p2))):
            dve.wait_ge(evac, 5 * t + (k + 2))
            if real(t - 1):
                dve.wait_ge(corr_ready, t - 1)
            nc.vector.tensor_tensor(dst[:, b], qs[:, b], ctx_part[:, b], ALU.mult).then_inc(prod, 1)

    def pe_corr(pe, t, b):
        pe.wait_ge(prod, 2 * t + 2)
        if real(t):
            pe.wait_ge(marked, t)
        if real(t):
            pe.wait_ge(less_done, t)
        for j in range(KT):
            ch, out_ = slice(j * P, (j + 1) * P), ps[:, CORR, j * P:(j + 1) * P]
            nc.tensor.matmul(out_, p1[:, b, ch], spec[:, INV_A], start=True, stop=False)
            mm = nc.tensor.matmul(out_, p2[:, b, ch], spec[:, INV_B], start=False, stop=True)
        mm.then_inc(corr_ready, 1)

    def rows(x, b):
        return x[:, b].rearrange("p (r l) -> p r l", l=L)

    def dve_top(dve, t, b):
        corr = ps[:, CORR].rearrange("p (r l) -> p r l", l=L)
        by_themselves(dve, t + 1, 2 * (t - 1))
        dve.wait_ge(corr_ready, t + 1)
        if real(2 * (t - 1)):
            dve.wait_ge(exp_done, 2 * (t - 1))
        for r in range(8):
            mm = nc.vector.max(top[:, b, r], corr[:, r])
        mm.then_inc(top_done, 1)
        largest = top[:, b, :, 0:1]
        dve.wait_ge(top_done, t + 1)
        nc.vector.tensor_tensor(topd[:, b], top[:, b], largest.to_broadcast([P, 8, TOPK]),
                                ALU.subtract).then_inc(topd_done, 1)
        nc.vector.tensor_tensor(rows(cd, b), corr, largest.to_broadcast([P, 8, L]),
                                ALU.subtract).then_inc(less_done, 1)
        by_themselves(dve, t - 1)
        if real(t - 1):
            dve.wait_ge(weighed, t - 1)
        for r in range(8):
            mm = nc.vector.match_replace(rows(mark, b)[:, r], top[:, b, r], corr[:, r], MARK)
        mm.then_inc(marked, 1)

    def act_exp(act, t, b):
        act.wait_ge(topd_done, t + 1)
        flat = topd[:, b].rearrange("p r k -> p (r k)")
        nc.scalar.activation(flat, flat, ACT.Exp).then_inc(exp_done, 1)
        act.wait_ge(less_done, t + 1)
        if real(t - 1):
            act.wait_ge(divided, t - 1)
        nc.scalar.activation(ex[:, b], cd[:, b], ACT.Exp).then_inc(exp_done, 1)

    def dve_sum(dve, t, b):
        dve.wait_ge(exp_done, 2 * t + 1)
        if real(t - 1):
            dve.wait_ge(divided, t - 1)
        nc.vector.tensor_reduce(zs[:, b], topd[:, b], AX.X, ALU.add).then_inc(summed, 1)
        dve.wait_ge(summed, 2 * t + 1)
        nc.vector.reciprocal(rz[:, b], zs[:, b]).then_inc(summed, 1)

    def pool_divide(pool, t, b):
        pool.wait_ge(exp_done, 2 * t + 2)
        pool.wait_ge(summed, 2 * t + 2)
        if real(t - 1):
            pool.wait_ge(weighed, t - 1)
        nc.gpsimd.tensor_tensor(rows(en, b), rows(ex, b), rz[:, b].unsqueeze(2).to_broadcast([P, 8, L]),
                                ALU.mult).then_inc(divided, 1)

    def dve_weigh(dve, t, b):
        dve.wait_ge(divided, t + 1)
        dve.wait_ge(marked, t + 1)
        if real(t - 1):
            dve.wait_ge(lag_turned, t - 1)
        nc.vector.scalar_tensor_tensor(out=wl[:, b], in0=mark[:, b], scalar=MARK, in1=en[:, b],
                                       op0=ALU.is_equal, op1=ALU.mult).then_inc(weighed, 1)

    def pe_lags(pe, t, b):
        pe.wait_ge(weighed, t + 1)
        if real(t):
            pe.wait_ge(x3_done, t)
        for j in range(KT):
            ch = slice(j * P, (j + 1) * P)
            mm = nc.tensor.transpose(ps[:, LAGS, ch], wl[:, b, ch], eye[:])
        mm.then_inc(lag_turned, 1)
        pe.wait_ge(lag_copied, t + 1)
        if real(2 * t):
            pe.wait_ge(pcyc, 2 * t)
        nc.tensor.matmul(ps[:, WCYC], spec[:, SPEC], wts[:, b], start=True, stop=True).then_inc(wspec, 1)
        if real(t):
            pe.wait_ge(wneg_copied, t)
        nc.tensor.matmul(ps[:, WNEG], spec[:, NEG], wts[:, b], start=True, stop=True).then_inc(wspec, 1)

    def act_lags(act, t, b):
        act.wait_ge(lag_turned, t + 1)
        if real(2 * (t - 1)):
            act.wait_ge(wspec, 2 * (t - 1))
        nc.scalar.copy(wts[:, b], ps[:, LAGS]).then_inc(lag_copied, 1)
        act.wait_ge(wspec, 2 * t + 2)
        if real(2 * (t - 1)):
            act.wait_ge(pneg, 2 * (t - 1))
        nc.scalar.copy(wns[:, b], ps[:, WNEG]).then_inc(wneg_copied, 1)

    def dve_cyclic(dve, t, b):
        dve.wait_ge(wspec, 2 * t + 1)
        if real(t - 1):
            dve.wait_ge(gathered, t - 1)
        nc.vector.tensor_tensor(pc1[:, b], ps[:, WCYC], kre[:, b], ALU.mult).then_inc(pcyc, 1)
        nc.vector.tensor_tensor(pc2[:, b], ps[:, WCYC], kim[:, b], ALU.mult).then_inc(pcyc, 1)

    def pool_negacyclic(pool, t, b):
        pool.wait_ge(wneg_copied, t + 1)
        if real(t - 1):
            pool.wait_ge(gathered, t - 1)
        nc.gpsimd.tensor_tensor(pn1[:, b], wns[:, b], nre[:, b], ALU.mult).then_inc(pneg, 1)
        nc.gpsimd.tensor_tensor(pn2[:, b], wns[:, b], nim[:, b], ALU.mult).then_inc(pneg, 1)

    def pe_gather(pe, t, b):
        parts = ((OUT_A, pc1, pcyc, 1), (OUT_B, pc2, pcyc, 2), (OUT_NA, pn1, pneg, 1),
                 (OUT_NB, pn2, pneg, 2))
        pe.wait_ge(lag_copied, t + 1)
        for k, (mat, src, ready, n) in enumerate(parts):
            pe.wait_ge(ready, 2 * t + n)
            mm = nc.tensor.matmul(ps[:, LAGS], spec[:, mat], src[:, b], start=(k == 0), stop=(k == 3))
        mm.then_inc(gathered, 1)

    def dve_x3(dve, t, b):
        dve.wait_ge(gathered, t + 1)
        if real(t - 1):
            dve.wait_ge(fin_done, t - 1)
        nc.vector.tensor_tensor(x3[:, b], tile_of(acc, t), ps[:, LAGS], ALU.add).then_inc(x3_done, 1)

    def pe_turn_h(pe, t, b):
        pe.wait_ge(xh3_done, t + 1)
        if real(t):
            pe.wait_ge(fin_done, t)
        for j in range(KT):
            ch = slice(j * P, (j + 1) * P)
            mm = nc.tensor.transpose(ps[:, MISC, ch], xh3[:, b, ch], eye[:])
        mm.then_inc(h_turned, 1)

    def act_turn_h(act, t, b):
        act.wait_ge(h_turned, t + 1)
        if real(t - 1):
            act.wait_ge(routed_in, t - 1)
        nc.scalar.copy(x3t[:, b], ps[:, MISC]).then_inc(h_copied, 1)

    def pe_route(pe, t, b):
        pe.wait_ge(h_copied, t + 1)
        if real(t):
            pe.wait_ge(wh_copied, t)
        for j in range(KT):
            mm = nc.tensor.matmul(ps[:, ROUTE, 0:P + E], x3t[:, b, j * P:(j + 1) * P], rt[:, j],
                                  start=(j == 0), stop=(j == KT - 1))
        mm.then_inc(routed_in, 1)

    def dve_route(dve, t, b):
        logits = ps[:, ROUTE, P:P + E]
        n = 4 * t
        by_themselves(dve, t + 1, 4 * (t - 1))
        dve.wait_ge(routed_in, t + 1)
        if real(4 * (t - 1)):
            dve.wait_ge(route, 4 * (t - 1))
        nc.vector.max(mx[:, b], logits).then_inc(route, 1)
        dve.wait_ge(route, n + 1)
        dve.wait_ge(prio_set, E)
        nc.vector.scalar_tensor_tensor(out=sc[:, b], in0=logits, scalar=mx[:, b, 0:1], in1=prio[:],
                                       op0=ALU.is_equal, op1=ALU.mult).then_inc(route, 1)
        by_themselves(dve, n + 2)
        dve.wait_ge(route, n + 2)
        nc.vector.max(m2[:, b], sc[:, b]).then_inc(route, 1)
        dve.wait_ge(route, n + 3)
        nc.vector.tensor_scalar(rw[:, b], sc[:, b], m2[:, b, 0:1], mx[:, b, 0:1], ALU.is_equal,
                                ALU.mult).then_inc(route, 1)
        dve.wait_ge(route, n + 4)
        if real(t - 1):
            dve.wait_ge(wh_turned, t - 1)
        nc.vector.tensor_tensor(wh[:, b].rearrange("p (e r) -> p e r", e=E),
                                ps[:, ROUTE, 0:P].rearrange("p (e r) -> p e r", e=E),
                                rw[:, b].unsqueeze(2).to_broadcast([P, E, R]),
                                ALU.mult).then_inc(wh_done, 1)

    def pe_turn_wh(pe, t, b):
        pe.wait_ge(wh_done, t + 1)
        nc.tensor.transpose(ps[:, ROUTE, 2 * P:3 * P], wh[:, b], eye[:]).then_inc(wh_turned, 1)

    def pe_expert(pe, t, b):
        pe.wait_ge(wh_copied, t + 1)
        pe.wait_ge(h_copied, t + 1)
        nc.tensor.matmul(ps[:, MISC], wht[:, b], eb[:], start=True, stop=True).then_inc(expert, 1)

    def act_expert(act, t, b):
        act.wait_ge(wh_turned, t + 1)
        if real(t - 1):
            act.wait_ge(expert, t - 1)
        nc.scalar.copy(wht[:, b], ps[:, ROUTE, 2 * P:3 * P]).then_inc(wh_copied, 1)

    def dve_final(dve, t, b, h):
        dve.wait_ge(expert, t + 1)
        if not isinstance(t, int) or t >= 2:
            dve.wait_ge(out_s[b], 16 * h)
        nc.vector.tensor_tensor(fin[:, b], x3[:, b], ps[:, MISC], ALU.add).then_inc(fin_done, 1)

    def sp_store(sp, t, b):
        sp.wait_ge(fin_done, t + 1)
        sp.dma_start(row_of(out, t), fin[:, b]).then_inc(out_s[b], 16)

    DEEP = 3

    PEEL = 6

    def slots(e, piece):
        def slot(v, par, hv):
            def at(stage):
                b = (par - stage) % 2
                h = hv + (par - stage - b) // 2
                t = 2 * h + b
                return None if isinstance(t, int) and not 0 <= t < TT else (t, b, h)
            piece(at)
        for v in range(PEEL):
            slot(v, v % 2, v // 2)
        with e.Fori(0, (TT - PEEL) // 2) as it:
            for k in range(2):
                slot(None, k, it + PEEL // 2)
        for v in range(TT, TT + DEEP):
            slot(v, v % 2, v // 2)

    LEAD = ATT + PER

    with nc.Block() as block:

        @block.sync
        def _(sp):
            sp_unit(sp, 0, 0, rows=False)
            sp_unit(sp, 0, 1, rows=False)
            sp.dma_start(nat_scale[:], scale_nat).then_inc(nat_in, 16)
            sp.dma_start(eye[:], eye_in).then_inc(eye_in_s, 16)
            sp.wait_ge(zeroed, 4)
            sp.dma_start(lattn[0:3 * R, 0:2, :], lora_attn[0]).then_inc(lora_in, 16)
            sp.dma_start(lattn[0:R, 2:4, :], lora_attn[1][0:R]).then_inc(lora_in, 16)
            sp.dma_start(lh[0:R], lora_h).then_inc(lora_in, 16)
            sp.dma_start(ldown[0:R], lora_down_b).then_inc(lora_in, 16)
            for b in range(2):
                sp.dma_start(lft[0:R, b, :], lora_ft[b]).then_inc(lft_in[b], 16)
            for c in range(NCH):
                src = x[SUB * c:SUB * (c + 1)].rearrange("s p d -> p s d")
                sp.dma_start(acc[:, SUB * c:SUB * (c + 1)], src).then_inc(x_in[c], 16)
            for v in range(2, LEAD):
                sp_unit(sp, v // 2, v % 2, rows=v >= NAT)

            def body(g, gp, m, ahead):
                if ahead:
                    for k in range(PER):
                        if k % 3 == 0:
                            lft_load(sp, g * 2 + (2 + k // 3), k // 3)
                        sp_unit(sp, *unit(m, k))
            pairs(sp, body)
            sp.wait_ge(lo_done, PER * NG)
            for dst, src in ((spec, spectral), (rt, router), (eb, expert_b)):
                sp.dma_start(dst[:], src).then_inc(const_in, 16)

            def piece(at):
                if a := at(0):
                    sp_ctx(sp, a[0], a[1])
                if a := at(3):
                    sp_store(sp, a[0], a[1])
            slots(sp, piece)
            for b in range(2):
                sp.wait_ge(out_s[b], 16 * TT // 2)

        @block.gpsimd
        def _(pool):
            for k, buf in enumerate((lattn, lh, lft, ldown)):
                nc.gpsimd.memset(buf[:], 0.0).then_inc(zeroed, 1)
            nc.gpsimd.memset(half[:], -0.5).then_inc(started, 1)
            pool.wait_ge(started, 1)
            for v in range(LEAD):
                pool_centre(pool, v // 2, v % 2)
                if v >= 1:
                    pool_scale(pool, (v - 1) // 2, (v - 1) % 2, nat=v - 1 if v - 1 < NAT else None)
                if v - 2 >= ATT:
                    pool_lo(pool, (v - 2) // 2, v % 2, 0, v - 2 - ATT)
                if v % SUB == 2 and v // SUB < NCH:
                    x_pow(pool, v // SUB)
                if v == ATT + 3:
                    pool_mt(pool)

            def body(g, gp, m, ahead):
                for c in range(NCH):
                    for i in range(2):
                        if ahead and i < len(SLOTS[c]):
                            k = SLOTS[c][i]
                            pool_centre(pool, *unit(m, k))
                            pool_scale(pool, *unit(m, k - 1))
                            _, wp, wk = place_of(g + 1, 1 - gp, k - 2)
                            pool_lo(pool, *unit(m, k - 2), wp, wk)
                        if not ahead and c == 0 and i == 0:
                            pool_scale(pool, *unit(m, -1))
                            pool_lo(pool, *unit(m, -2), gp, PER - 2)
                            pool_lo(pool, *unit(m, -1), gp, PER - 1)
                        pool_hlo(pool, g, c, i)
            pairs(pool, body)
            for k in range(E):
                nc.gpsimd.memset(prio[:, k:k + 1], float(E - k)).then_inc(prio_set, 1)

            def piece(at):
                if a := at(0):
                    pool_pow(pool, 2, *a[:2])
                if a := at(2):
                    pool_divide(pool, *a[:2])
                    pool_negacyclic(pool, *a[:2])
                    pool_pow(pool, 3, *a[:2])
            slots(pool, piece)

        @block.scalar
        def _(act):
            for k in range(2 * KT):
                act.wait_ge(al_ready, k + 1)
                dst = wsum[:, k] if k < KT else w3[:, k - KT]
                nc.scalar.copy(dst, ps[:, k % KT]).then_inc(al_copied, 1)
            for v in range(LEAD):
                act_lines(act, v // 2, v % 2)
                if v - 2 >= ATT:
                    act_hi(act, (v - 2) // 2, v % 2, 0, 0, v - 2 - ATT)
                if SUB <= v < SUB + TT:
                    x_normalise(act, v - SUB)
                    x_hi_copy(act, v - SUB)
                if v == ATT + 3:
                    act_mt(act)
            for c in range(NCH):
                act_x1(act, c)

            def body(g, gp, m, ahead):
                for c in range(NCH):
                    for i in range(2):
                        if ahead and i < len(SLOTS[c]):
                            k = SLOTS[c][i]
                            act_lines(act, *unit(m, k))
                            wg, wp, wk = place_of(g + 1, 1 - gp, k - 2)
                            act_hi(act, *unit(m, k - 2), wp, wg, wk)
                        if not ahead and c == 0 and i == 0:
                            act_hi(act, *unit(m, -2), gp, g, PER - 2)
                            act_hi(act, *unit(m, -1), gp, g, PER - 1)
                        act_silu(act, g, c, i)
                        act_hhi(act, g, c, i)
            pairs(act, body)
            act.wait_ge(added, 4 * NCH * NG)

            def piece(at):
                if a := at(1):
                    act_evac(act, *a[:2])
                if a := at(3):
                    act_turn_h(act, *a[:2])
                if a := at(2):
                    act_exp(act, *a[:2])
                if a := at(3):
                    act_expert(act, *a[:2])
                if a := at(2):
                    act_lags(act, *a[:2])
            slots(act, piece)

        @block.vector
        def _(dve):
            dve.wait_ge(started, 1)
            for v in range(LEAD):
                if v >= 1:
                    dve_mix(dve, (v - 1) // 2, (v - 1) % 2)
                if v >= 2:
                    u = v - 2
                    dve_fold(dve, u // 2, u % 2, u if u < ATT else None)
                c, s = divmod(v - 2, SUB)
                if s == 0 and 0 <= c < NCH:
                    x_stats(dve, c)
                if s == 1 and 0 <= c < NCH:
                    x_rstd(dve, c)
                if SUB <= v < SUB + TT:
                    x_lo_sub(dve, v - SUB)
                if v == ATT + 3:
                    dve_mt(dve)
            for c in range(NCH):
                dve_x1(dve, c)

            def body(g, gp, m, ahead):
                for c in range(NCH):
                    for i in range(2):
                        if ahead and i < len(SLOTS[c]):
                            k = SLOTS[c][i]
                            dve_mix(dve, *unit(m, k - 1))
                            dve_fold(dve, *unit(m, k - 2))
                        if not ahead and c == 0 and i == 0:
                            dve_mix(dve, *unit(m, -1))
                            dve_fold(dve, *unit(m, -2))
                            dve_fold(dve, *unit(m, -1))
                        dve_hmul(dve, g, c, i)
                    if c > 0:
                        dve_add(dve, g, c - 1)
                    elif not (isinstance(g, int) and g == 0):
                        dve_add(dve, g - 1, NCH - 1)
            pairs(dve, body)
            dve_add(dve, NG - 1, NCH - 1)
            dve.wait_ge(added, 4 * NCH * NG)

            def piece(at):
                if a := at(3):
                    dve_normalise(dve, 3, x3[:, a[1]], xh3[:, a[1]], *a[:2])
                if a := at(0):
                    dve_stats(dve, 2, tile_of(acc, a[0]), *a[:2])
                if a := at(2):
                    dve_top(dve, *a[:2])
                if a := at(1):
                    dve_products(dve, *a[:2])
                if a := at(2):
                    dve_sum(dve, *a[:2])
                if a := at(3):
                    dve_route(dve, *a[:2])
                if a := at(2):
                    dve_weigh(dve, *a[:2])
                if a := at(0):
                    dve_normalise(dve, 2, tile_of(acc, a[0]), xq[:, a[1]], *a[:2])
                if a := at(2):
                    dve_cyclic(dve, *a[:2])
                if a := at(3):
                    dve_final(dve, *a)
                if a := at(2):
                    dve_x3(dve, *a[:2])
                    dve_stats(dve, 3, x3[:, a[1]], *a[:2])
            slots(dve, piece)

        @block.tensor
        def _(pe):
            pe.wait_ge(zeroed, 4)
            pe.wait_ge(lora_in, 64)
            for k in range(2 * KT):
                if real(k - KT + 1):
                    pe.wait_ge(al_copied, k - KT + 1)
                rows_ = slice((k % KT) * P, (k % KT + 1) * P)
                lhs, rhs = ((lattn[:, 1, rows_], lattn[:, 0]) if k < KT else
                            (lattn[:, 2, rows_], lattn[:, 3]))
                nc.tensor.matmul(ps[:, k % KT], lhs, rhs, start=True, stop=True).then_inc(al_ready, 1)
            for v in range(LEAD):
                if v - 1 >= ATT:
                    pe_lora(pe, (v - 1) // 2, (v - 1) % 2, 0, v - 1 - ATT)
                if SUB <= v < SUB + TT:
                    x_turn(pe, v - SUB)
                if v == ATT + 2:
                    pe_mt(pe)
            for c in range(NCH):
                pe_x1(pe, c)
                pe_x1_turn(pe, c)

            def body(g, gp, m, ahead):
                for c in range(NCH):
                    pe_gate_up(pe, g, gp, c, (0,))
                    if ahead:
                        for k in SLOTS[c]:
                            wg, wp, wk = place_of(g + 1, 1 - gp, k - 1)
                            pe_lora(pe, *unit(m, k - 1), wg, wk)
                    elif c == 0:
                        pe_lora(pe, *unit(m, -1), g, PER - 1)
                    pe_gate_up(pe, g, gp, c, (1,))
                    if c > 0:
                        pe_down(pe, g, gp, c - 1)
                    elif not (isinstance(g, int) and g == 0):
                        pe_down(pe, g - 1, 1 - gp, NCH - 1)
            pairs(pe, body)
            pe_down(pe, NG - 1, 0, NCH - 1)

            def piece(at):
                if a := at(1):
                    pe_forward(pe, *a)
                if a := at(3):
                    pe_turn_h(pe, *a[:2])
                if a := at(1):
                    pe_corr(pe, *a[:2])
                if a := at(3):
                    pe_route(pe, *a[:2])
                    pe_turn_wh(pe, *a[:2])
                if a := at(2):
                    pe_lags(pe, *a[:2])
                if a := at(3):
                    pe_expert(pe, *a[:2])
                if a := at(2):
                    pe_gather(pe, *a[:2])
            slots(pe, piece)
    st.close()


def kernel(x, ctx_4096, L0_attn_codes_attn, L0_attn_scales_attn, L0_attn_codes_gu,
           L0_attn_scales_gu, L0_attn_codes_down, L0_attn_scales_down, L0_attn_lora_A_h,
           L0_attn_lora_A_down, L0_attn_lora_B_attn, L0_attn_lora_B_gu, L0_attn_lora_B_down,
           L0_ffn_route_w, L0_ffn_A, L0_ffn_Bw):
    import concourse.bacc as bacc
    from concourse.bass_utils import run_bass_kernel_spmd

    arr = lambda a: np.asarray(a)
    ca, cgu, cd = arr(L0_attn_codes_attn), arr(L0_attn_codes_gu), arr(L0_attn_codes_down)
    sa, sgu, sd = arr(L0_attn_scales_attn), arr(L0_attn_scales_gu), arr(L0_attn_scales_down)
    ah, ad = arr(L0_attn_lora_A_h), arr(L0_attn_lora_A_down)
    ba, bgu, bd = arr(L0_attn_lora_B_attn), arr(L0_attn_lora_B_gu), arr(L0_attn_lora_B_down)
    nat = ca[:3].reshape(NAT, P, D)
    tr = ca[3].T.reshape(KT, P, D)
    gu = cgu.reshape(2, NFT, P, KT, P).transpose(1, 0, 4, 3, 2).reshape(NFT, 2, P, D)
    dn = cd.T.reshape(NFT, 1, P, D)
    ft = np.concatenate([gu, dn], axis=1).reshape(3 * NFT, P, D)
    codes = np.concatenate([nat, tr, ft])
    scale_nat = sa[:3].reshape(NAT, P, D // QB).transpose(1, 0, 2)
    s_tr = sa[3].T.reshape(KT, 2, D)
    s_gu = sgu.reshape(2, NFT, P, KT, 2).transpose(1, 0, 4, 3, 2).reshape(NFT, 2, 2, D)
    s_dn = sd.T.reshape(NFT, 1, 2, D)
    s_ft = np.concatenate([s_gu, s_dn], axis=1).reshape(3 * NFT, 2, D)
    scale_rows = np.concatenate([s_tr, s_ft]).reshape(-1, 1, D)
    lora_attn = np.zeros((2, 3 * R, 2, D), np.float32)
    lora_attn[0, :, 0] = ah[:3].reshape(3 * R, D)
    lora_attn[0, :, 1] = ba[:3].transpose(0, 2, 1).reshape(3 * R, D)
    lora_attn[1, :R, 0] = ah[3]
    lora_attn[1, :R, 1] = ba[3].T
    lora_h = ah[4:6].transpose(1, 0, 2)
    b_t = bgu.reshape(2, NFT, P, R).transpose(1, 3, 0, 2).reshape(NFT, R, 2 * P)
    a_t = ad.reshape(R, NFT, P).transpose(1, 0, 2)
    lora_ft = np.concatenate([b_t, a_t], axis=2)
    cols = np.concatenate([arr(L0_ffn_A).reshape(P, D), arr(L0_ffn_route_w)]).T
    router = cols.reshape(KT, P, P + E).transpose(1, 0, 2)
    expert_b = arr(L0_ffn_Bw).transpose(0, 2, 1).reshape(P, D)
    given = {
        "x": arr(x).reshape(TT, P, D), "ctx": arr(ctx_4096).reshape(TT, P, D), "codes": codes,
        "scale_nat": scale_nat, "scale_rows": scale_rows, "lora_attn": lora_attn,
        "lora_h": lora_h, "lora_ft": lora_ft, "lora_down_b": bd.T, "router": router,
        "expert_b": expert_b, "spectral": spectral_matrices(), "eye": np.eye(P, dtype=np.float32),
    }
    given = {f"in_{k}": np.ascontiguousarray(v) for k, v in given.items()}
    nc = bacc.Bacc("TRN2", target_bir_lowering=False, num_devices=1)
    args = [nc.dram_tensor(k, v.shape, mybir.dt.from_np(v.dtype), kind="ExternalInput").ap()
            for k, v in given.items()]
    out = nc.dram_tensor("out", (TT, P, D), F32, kind="ExternalOutput").ap()
    build(nc, *args, out)
    r = run_bass_kernel_spmd(nc, [given], core_ids=[0])
    return r.results[0]["out"].reshape(SEQS, L, D)
```

```python
from contextlib import ExitStack

import concourse.bass as bass
import numpy as np
from concourse import mybir

F32 = mybir.dt.float32
F32R = mybir.dt.float32r
I32 = mybir.dt.int32
ALU = mybir.AluOpType
ACT = mybir.ActivationFunctionType
AX = mybir.AxisListType

P = 128
D = 512
KT = D // P
SEQS, L = 32, 64
T = SEQS * L
TT = T // P
CH = 512
NCH = T // CH
SUB = CH // P
FF = 1792
NFT = FF // P
NG = NFT // 2
QB = 64
R = 16
E = 8
TOPK = int(2 * np.log(L))
assert TOPK == 8 and D == CH
EPS = 1e-5
MARK = -3.0e38

ATT = 4 * KT
NAT = ATT - KT
PER = 6
UNITS = ATT + PER * NG

LINES = [(0.30380717, 1.1266502),
         (0.0851821, -0.009434006),
         (0.13015553, 0.12570463),
         (0.10279457, -0.07326305),
         (0.099667944, 0.0145624615),
         (0.16033982, -0.3994219)]
NL = len(LINES)
SLOPE_LOW = 0.09105003625154495
SLOPE_HIGH = 0.07958029955625534
LAST = (0.5, -3.0)
MIX = 8

SPEC, KRE, KIM, NEG, NRE, NIM, INV_A, INV_B, OUT_A, OUT_B, OUT_NA, OUT_NB = range(12)


def spectral_matrices():
    n = np.arange(L)
    th = 2 * np.pi / L
    re, im, odd = np.arange(L // 2 + 1), np.arange(1, L // 2), np.arange(L // 2) + 0.5
    cos = lambda f: np.cos(th * np.outer(f, n))
    sin = lambda f: np.sin(th * np.outer(f, n))
    two = lambda a, b: np.vstack([a, b])
    spec = two(cos(re), -sin(im))
    kre = two(cos(re), cos(im))
    kre[0, L - 1] += L
    kim = two(-sin(re), -sin(im))
    kim[0], kim[L // 2] = 1, 0
    neg = two(cos(odd), -sin(odd))
    less_last = np.eye(L)
    less_last[:, L - 1] -= 1
    nre = two(cos(odd), cos(odd)) @ less_last
    nim = two(-sin(odd), -sin(odd)) @ less_last
    c = np.full((L // 2 + 1, 1), 2 / L)
    c[0] = c[-1] = 1 / L
    ci = 2 / L
    inv_a = two(c * cos(re), -ci * sin(im))
    inv_a[0] = 0
    inv_b = two(c * sin(re), ci * cos(im))
    inv_b[0] = 1 / L
    out_a = two(c * cos(re), ci * sin(im)) / 2
    out_b = two(-c * sin(re), ci * cos(im)) / 2
    out_b[0] = 0
    out_na = two(cos(odd), sin(odd)) * ci / 2
    out_nb = two(-sin(odd), cos(odd)) * ci / 2
    forward = [m.T for m in (spec, kre, kim, neg, nre, nim)]
    mats = forward + [inv_a, inv_b, out_a, out_b, out_na, out_nb]
    both = np.zeros((P, len(mats), P), np.float32)
    for k, m in enumerate(mats):
        both[:L, k, :L] = m
        both[L:, k, L:] = m
    return both



def build(nc, x, ctx_in, codes, scale_nat, scale_rows, lora_attn, lora_h, lora_ft, lora_down_b,
          router, expert_b, spectral, eye_in, out):
    st = ExitStack()
    sem = lambda name: st.enter_context(nc.semaphore(name))

    place = {"at": nc.sbuf_base}

    def sb(name, shape, dt=F32, at=None):
        if at is not None:
            place["at"] = at
        start = -(-place["at"] // 32) * 32
        place["at"] = start + 4 * int(np.prod(shape[1:]))
        return nc.alloc_sbuf_tensor_at(name, shape, dt, offset=start)

    acc = sb("acc", [P, TT, D])
    eye = sb("eye", [P, P])
    stats = sb("stats", [P, SUB, 6])
    mv = sb("mv", [P, SUB, 2])
    ve = sb("ve", [P, SUB])
    pw = sb("pw", [P, SUB])
    nt = sb("nt", [P, 2, SUB])
    rstd = sb("rstd", [P, NCH, SUB])
    nmr = sb("nmr", [P, NCH, SUB])
    half = sb("half", [P, SUB])
    eye3 = sb("eye3", [P, P])
    dq_at = place["at"]
    codes_sb = sb("codes_sb", [P, 2, CH], I32)
    scale_sb = sb("scale_sb", [P, 2, CH])
    xc = sb("xc", [P, 2, CH])
    line = sb("line", [P, NL, CH])
    last_line = sb("last_line", [P, CH])
    wt = sb("wt", [P, 2, CH])
    ldown = sb("ldown", [P, D])
    lh = sb("lh", [P, 2, P])
    lft = sb("lft", [P, 2, 2 * CH + P])
    nat_scale = sb("nat_scale", [P, NAT, D // QB])
    dq_end = place["at"]
    x_hi = sb("x_hi", [P, KT, T], F32R)
    x_lo = sb("x_lo", [P, KT, T], F32R)
    w0_at = place["at"]
    w_hi = [sb("w_hi0", [P, PER, CH], F32R)]
    w_lo = [sb("w_lo0", [P, PER, CH], F32R)]
    w1_at = place["at"]
    w_hi.append(sb("w_hi1", [P, PER, CH], F32R))
    w_lo.append(sb("w_lo1", [P, PER, CH], F32R))
    h_at = place["at"]
    h_hi = sb("h_hi", [P, 2, 2, CH], F32R)
    h_lo = sb("h_lo", [P, 2, 2, CH], F32R)
    hf = sb("hf", [P, 2, CH])
    end_b = place["at"]
    wsum = sb("wsum", [P, KT, D], at=w1_at)
    w3 = sb("w3", [P, KT, D])
    lattn = sb("lattn", [P, 4, D])
    x1f = sb("x1f", [P, 2, CH], at=w1_at)
    mt_hi = sb("mt_hi", [P, KT, D], F32R, at=h_at)
    mt_lo = sb("mt_lo", [P, KT, D], F32R)
    xhat = sb("xhat", [P, 2, D])
    two = lambda name, shape=(D,), at=None: sb(name, [P, 2, *shape], at=at)
    spec = sb("spec", [P, 12, P], at=dq_at)
    rt = sb("rt", [P, KT, P + E])
    eb = sb("eb", [P, D])
    prio = sb("prio", [P, E])
    ctx = sb("ctx", [P, 2, D])
    lst = {k: (sb(f"st{k}", [P, 2, 6]), sb(f"mv{k}", [P, 2, 2]), sb(f"ve{k}", [P, 2]),
               sb(f"pw{k}", [P, 2]), sb(f"na{k}", [P, 2]), sb(f"nb{k}", [P, 2]),
               sb(f"rs{k}", [P, 2])) for k in (2, 3)}
    xq = two("xq")
    qs = two("qs")
    p1, p2 = two("p1"), two("p2")
    ct = two("ct")
    assert place["at"] <= dq_end
    kre, kim, nre, nim = two("kre", at=w1_at), two("kim"), two("nre"), two("nim")
    assert place["at"] <= h_at
    top = two("top", (8, TOPK), at=dq_end)
    topd = two("topd", (8, TOPK))
    cd = two("cd")
    ex = two("ex")
    mark = two("mark")
    zs, rz = two("zs", (8,)), two("rz", (8,))
    en = two("en")
    wl = two("wl")
    wts = two("wts")
    wns = two("wns")
    pc1, pc2, pn1, pn2 = two("pc1"), two("pc2"), two("pn1"), two("pn2")
    x3 = two("x3")
    xh3 = two("xh3")
    x3t = two("x3t")
    mx, sc, m2, rw = two("mx", (8,)), two("sc", (E,)), two("m2", (8,)), two("rw", (E,))
    wh, wht = two("wh", (P,)), two("wht", (P,))
    assert place["at"] <= w0_at
    fin = two("fin", at=h_at)
    assert max(end_b, place["at"]) <= nc.sbuf_usable_end
    ps = st.enter_context(nc.psum_tensor("ps", [P, 8, CH], F32))
    CORR, LAGS, WCYC, WNEG, MISC, ROUTE, FWD = range(7)

    started = sem("started")
    zeroed = sem("zeroed")
    eye_in_s, lora_in, nat_in = sem("eye_in"), sem("lora_in"), sem("nat_in")
    x_in = [sem(f"x_in{k}") for k in range(NCH)]
    codes_in = [sem(f"codes_in{k}") for k in range(2)]
    scales_in = [sem(f"scales_in{k}") for k in range(2)]
    lft_in = [sem(f"lft_in{k}") for k in range(2)]
    centred, lined, last_lined = sem("centred"), sem("lined"), sem("last_lined")
    att_folded = sem("att_folded")
    mixed, scaled, folded = sem("mixed"), sem("scaled"), sem("folded")
    hi_done, lo_done, lora_ready = sem("hi_done"), sem("lo_done"), sem("lora_ready")
    al_ready, al_copied = sem("al_ready"), sem("al_copied")
    ln1, pow1 = sem("ln1"), sem("pow1")
    normed, turned, xhi_done, xlo_done = sem("normed"), sem("turned"), sem("xhi"), sem("xlo")
    eye3_made, mt_ready, mt_hi_done, mt_lo_done = (sem("eye3_made"), sem("mt_ready"),
                                                   sem("mt_hi_done"), sem("mt_lo_done"))
    x1_ready, x1_copied, x1_hi, x1_lo = sem("x1_ready"), sem("x1_copied"), sem("x1_hi"), sem("x1_lo")
    x1_turned, x1_added = sem("x1_turned"), sem("x1_added")
    gu, silu_done, hmul_done = sem("gu"), sem("silu_done"), sem("hmul_done")
    hhi_done, hlo_done, down, added = sem("hhi_done"), sem("hlo_done"), sem("down"), sem("added")

    def real(n):
        return not isinstance(n, int) or n > 0

    def by_themselves(e, *counts):
        for n in counts:
            if real(n):
                e.compute_val(n)
        e.wait_ge(started, 1)

    def sp_unit(sp, m, b, rows=True):
        u = 2 * m + b
        if real(u - 1):
            sp.wait_ge(centred, u - 1)
        sp.dma_start(codes_sb[:, b, :], row_of(codes, u)).then_inc(codes_in[b], 16)
        if rows:
            if real(u - 1):
                sp.wait_ge(scaled, u - 1)
            for h in range(2):
                row = row_of(scale_rows, (2 * u if first(u) else 2 * u - 2 * NAT) + h)
                sp.dma_start(scale_sb[QB * h:QB * h + QB, b, :],
                             row.to_broadcast([QB, CH])).then_inc(scales_in[b], 16)

    def first(u):
        return isinstance(u, int) and u < KT

    def row_of(dram, n):
        return dram[n] if isinstance(n, int) else dram[bass.ds(n, 1)].rearrange("o p f -> (o p) f")

    def lft_load(sp, f, b):
        sp.wait_ge(lora_ready, 3 * (f - 1))
        lft_parts(sp, row_of(lora_ft, f), b)

    def lft_parts(sp, src, b):
        for kt in range(KT):
            dst = lft[kt * R:(kt + 1) * R, b, 0:2 * CH].rearrange("p (w k n) -> p w k n", w=2, k=KT)
            sp.dma_start(dst[:, :, kt], src[:, 0:2 * P].rearrange("p (w n) -> p w n", w=2)
                         ).then_inc(lft_in[b], 16)
        sp.dma_start(lft[0:R, b, 2 * CH:], src[:, 2 * P:]).then_inc(lft_in[b], 16)

    def pool_centre(pool, m, b):
        u = 2 * m + b
        by_themselves(pool, 16 * m + 16, NL * (u - 1), MIX * (u - 2) + 2)
        pool.wait_ge(codes_in[b], 16 * m + 16)
        if real(NL * (u - 1)):
            pool.wait_ge(lined, NL * (u - 1))
        if real(MIX * (u - 2) + 2):
            pool.wait_ge(mixed, MIX * (u - 2) + 2)
        nc.gpsimd.tensor_scalar(xc[:, b], codes_sb[:, b], -7.0, 1.0, ALU.add,
                                ALU.mult).then_inc(centred, 1)

    def pool_last(pool, m, b):
        u = 2 * m + b
        by_themselves(pool, u + 1, MIX * (u - 1) + 6)
        pool.wait_ge(centred, u + 1)
        if real(MIX * (u - 1) + 6):
            pool.wait_ge(mixed, MIX * (u - 1) + 6)
        nc.gpsimd.tensor_scalar(last_line[:], xc[:, b], LAST[0], LAST[1], ALU.mult,
                                ALU.add).then_inc(last_lined, 1)

    FREE_AFTER = [3, 4, 5, 7, 8, 8]

    def act_lines(act, m, b, some):
        u = 2 * m + b
        act.wait_ge(centred, u + 1)
        for k in some:
            s, c = LINES[k]
            if real(MIX * (u - 1) + FREE_AFTER[k]):
                act.wait_ge(mixed, MIX * (u - 1) + FREE_AFTER[k])
            nc.scalar.activation(line[:, k], xc[:, b], ACT.Identity, bias=c,
                                 scale=s).then_inc(lined, 1)

    EARLY, LATE = range(4), range(4, NL)

    def dve_mix(dve, m, b):
        u = 2 * m + b
        n, k = MIX * u, NL * u
        X = xc[:, b]
        dve.wait_ge(centred, u + 1)
        dve.wait_ge(lined, k + 1)
        nc.vector.scalar_tensor_tensor(out=line[:, 0], in0=X, scalar=SLOPE_LOW, in1=line[:, 0],
                                       op0=ALU.mult, op1=ALU.min).then_inc(mixed, 1)
        dve.wait_ge(lined, k + 2)
        nc.vector.scalar_tensor_tensor(out=line[:, 1], in0=X, scalar=SLOPE_HIGH, in1=line[:, 1],
                                       op0=ALU.mult, op1=ALU.max).then_inc(mixed, 1)
        dve.wait_ge(lined, k + 3)
        dve.wait_ge(mixed, n + 1)
        nc.vector.tensor_tensor(line[:, 2], line[:, 2], line[:, 0], ALU.min).then_inc(mixed, 1)
        dve.wait_ge(lined, k + 4)
        dve.wait_ge(mixed, n + 2)
        nc.vector.tensor_tensor(line[:, 3], line[:, 3], line[:, 1], ALU.max).then_inc(mixed, 1)

    def dve_mix_on(dve, m, b):
        u = 2 * m + b
        n, k = MIX * u, NL * u
        dve.wait_ge(lined, k + 5)
        dve.wait_ge(mixed, n + 3)
        nc.vector.tensor_tensor(line[:, 4], line[:, 4], line[:, 2], ALU.min).then_inc(mixed, 1)
        dve.wait_ge(lined, k + 6)
        dve.wait_ge(last_lined, u + 1)
        nc.vector.tensor_tensor(line[:, 5], line[:, 5], last_line[:], ALU.max).then_inc(mixed, 1)
        dve.wait_ge(mixed, n + 5)
        nc.vector.tensor_tensor(line[:, 4], line[:, 4], line[:, 3], ALU.min).then_inc(mixed, 1)
        dve.wait_ge(mixed, n + 7)
        if isinstance(u, int) and u < ATT + 2:
            if real(u - 1):
                dve.wait_ge(att_folded, u - 1)
        else:
            dve.wait_ge(lo_done, u - (1 + ATT))
        nc.vector.tensor_tensor(wt[:, b], line[:, 4], line[:, 5], ALU.max).then_inc(mixed, 1)

    def pool_scale(pool, m, b, nat=None):
        u = 2 * m + b
        pool.wait_ge(mixed, MIX * u + MIX)
        if nat is not None:
            pool.wait_ge(nat_in, 16)
            s = nat_scale[:, nat, :].unsqueeze(2).to_broadcast([P, D // QB, QB])
            w = wt[:, b].rearrange("p (a q) -> p a q", q=QB)
        else:
            pool.wait_ge(scales_in[b], 32 * (m if first(u) else m - NAT // 2) + 32)
            s, w = scale_sb[:, b], wt[:, b]
        nc.gpsimd.tensor_tensor(w, w, s, ALU.mult).then_inc(scaled, 1)

    def pe_lora(pe, m, b, g, k):
        u = 2 * m + b
        ft_b = k // 3
        if real(u - (ATT + 1)):
            pe.wait_ge(folded, u - (ATT + 1))
        if k % 3 == 0:
            pe.wait_ge(lft_in[ft_b], 16 * (KT + 1) * (g + 1))
        if k % 3 < 2:
            w = k % 3
            mm = nc.tensor.matmul(ps[:, 6 + b, :], lh[:, w], lft[:, ft_b, w * CH:(w + 1) * CH],
                                  start=True, stop=True)
        else:
            mm = nc.tensor.matmul(ps[:, 6 + b, :], lft[:, ft_b, 2 * CH:], ldown[:],
                                  start=True, stop=True)
        mm.then_inc(lora_ready, 1)

    def pool_fold(pool, u):
        o = (u - KT) // 3
        dst = w3[:, u] if u < KT else wsum[:, o]
        pool.wait_ge(scaled, u + 1)
        pool.wait_ge(al_copied, u + 1 if u < KT else KT + o + 1)
        if real(u):
            pool.wait_ge(att_folded, u)
        nc.gpsimd.tensor_tensor(dst, dst, wt[:, u % 2], ALU.add).then_inc(att_folded, 1)

    def dve_fold(dve, m, b):
        u = 2 * m + b
        dve.wait_ge(scaled, u + 1)
        dve.wait_ge(lora_ready, u - (ATT - 1))
        nc.vector.tensor_tensor(wt[:, b], wt[:, b], ps[:, 6 + b, :], ALU.add).then_inc(folded, 1)

    def act_hi(act, m, b, gp, g, k):
        u = 2 * m + b
        act.wait_ge(folded, u - (ATT - 1))
        if k == 0 and not (isinstance(g, int) and g == 0):
            act.wait_ge(x1_turned, KT * NCH)
            if real(4 * NCH * (g - 1)):
                act.wait_ge(down, 4 * NCH * (g - 1))
        nc.scalar.copy(w_hi[gp][:, k], wt[:, b]).then_inc(hi_done, 1)

    def pool_lo(pool, m, b, gp, k):
        u = 2 * m + b
        pool.wait_ge(hi_done, u - (ATT - 1))
        nc.gpsimd.tensor_tensor(w_lo[gp][:, k], wt[:, b], w_hi[gp][:, k].bitcast(F32),
                                ALU.subtract).then_inc(lo_done, 1)

    def x_stats(dve, c):
        n = LNS * c
        dve.wait_ge(x_in[c], 16)
        for s in range(SUB):
            nc.vector.bn_stats(stats[:, s], acc[:, SUB * c + s]).then_inc(ln1, 1)
        if real(n):
            dve.wait_ge(ln1, n)
        for s in range(SUB):
            dve.wait_ge(ln1, n + s + 1)
            nc.vector.bn_aggr(mv[:, s], stats[:, s]).then_inc(ln1, 1)
        dve.wait_ge(ln1, n + 2 * SUB)
        if real(c):
            dve.wait_ge(pow1, c)
        nc.vector.tensor_scalar(ve[:], mv[:, :, 1], EPS, None, ALU.add).then_inc(ln1, 1)

    LNS = 2 * SUB + 5

    def x_pow(pool, c):
        pool.wait_ge(ln1, LNS * c + 2 * SUB + 1)
        nc.gpsimd.tensor_tensor(pw[:], ve[:], half[:], ALU.pow).then_inc(pow1, 1)

    def newton(dve, count, n, v, y, t1, t2, r):
        nc.vector.tensor_tensor(t1, y, y, ALU.mult).then_inc(count, 1)
        dve.wait_ge(count, n + 1)
        nc.vector.scalar_tensor_tensor(out=t2, in0=t1, scalar=-0.5, in1=v, op0=ALU.mult,
                                       op1=ALU.mult).then_inc(count, 1)
        dve.wait_ge(count, n + 2)
        nc.vector.scalar_tensor_tensor(out=r, in0=t2, scalar=1.5, in1=y, op0=ALU.add,
                                       op1=ALU.mult).then_inc(count, 1)

    def x_rstd(dve, c):
        n = LNS * c + 2 * SUB + 1
        dve.wait_ge(pow1, c + 1)
        newton(dve, ln1, n, ve[:], pw[:], nt[:, 0], nt[:, 1], rstd[:, c])
        dve.wait_ge(ln1, n + 3)
        nc.vector.scalar_tensor_tensor(out=nmr[:, c], in0=mv[:, :, 0], scalar=-1.0, in1=rstd[:, c],
                                       op0=ALU.mult, op1=ALU.mult).then_inc(ln1, 1)

    def x_normalise(act, t):
        c, s = divmod(t, SUB)
        act.wait_ge(ln1, LNS * (c + 1))
        if real(t - 1):
            act.wait_ge(turned, t - 1)
        nc.scalar.activation(xhat[:, t % 2], acc[:, t], ACT.Identity, bias=nmr[:, c, s:s + 1],
                             scale=rstd[:, c, s:s + 1]).then_inc(normed, 1)

    def x_turn(pe, t):
        pe.wait_ge(eye_in_s, 16)
        pe.wait_ge(normed, t + 1)
        if real(t - 1):
            pe.wait_ge(xlo_done, t - 1)
        for kt in range(KT):
            mm = nc.tensor.transpose(ps[:, 4 + t % 2, kt * P:(kt + 1) * P],
                                     xhat[:, t % 2, kt * P:(kt + 1) * P], eye[:])
        mm.then_inc(turned, 1)

    def by_tile(xt, t):
        return xt[:, :, t * P:(t + 1) * P]

    def bank_tile(t):
        return ps[:, 4 + t % 2].rearrange("p (k n) -> p k n", k=KT)

    def x_hi_copy(act, t):
        act.wait_ge(turned, t + 1)
        nc.scalar.copy(by_tile(x_hi, t), bank_tile(t)).then_inc(xhi_done, 1)

    def x_lo_sub(dve, t):
        dve.wait_ge(xhi_done, t + 1)
        nc.vector.tensor_tensor(by_tile(x_lo, t), bank_tile(t), by_tile(x_hi, t).bitcast(F32),
                                ALU.subtract).then_inc(xlo_done, 1)

    def pe_mt(pe, o):
        pe.wait_ge(att_folded, KT + 3 * (o + 1))
        for kt in range(KT):
            if o == 0:
                pe.wait_ge(al_copied, 2 * KT)
            mm = nc.tensor.matmul(ps[:, kt, :], wsum[:, o, kt * P:(kt + 1) * P], w3[:, o],
                                  start=(o == 0), stop=False)
            if o == KT - 1:
                pe.wait_ge(eye3_made, 1)
                mm = nc.tensor.matmul(ps[:, kt, kt * P:(kt + 1) * P], eye[:], eye3[:],
                                      start=False, stop=True)
                mm.then_inc(mt_ready, 1)

    def act_mt(act):
        for kt in range(KT):
            act.wait_ge(mt_ready, kt + 1)
            nc.scalar.activation(mt_hi[:, kt], ps[:, kt], ACT.Identity,
                                 scale=1.0 / 3.0).then_inc(mt_hi_done, 1)

    def dve_mt(dve):
        for kt in range(KT):
            dve.wait_ge(mt_hi_done, kt + 1)
            nc.vector.scalar_tensor_tensor(out=mt_lo[:, kt], in0=ps[:, kt], scalar=1.0 / 3.0,
                                           in1=mt_hi[:, kt].bitcast(F32), op0=ALU.mult,
                                           op1=ALU.subtract).then_inc(mt_lo_done, 1)

    def three(pe, bank, hi, lo, rhs_hi, rhs_lo, start, stop):
        nc.tensor.matmul(bank, hi, rhs_hi, start=start, stop=False)
        nc.tensor.matmul(bank, hi, rhs_lo, start=False, stop=False)
        return nc.tensor.matmul(bank, lo, rhs_hi, start=False, stop=stop)

    def pe_x1(pe, n):
        c, f = divmod(n, KT)
        chunk = slice(c * CH, (c + 1) * CH)
        pe.wait_ge(mt_lo_done, KT)
        pe.wait_ge(xlo_done, SUB * (c + 1))
        if real(n - KT + 1):
            pe.wait_ge(x1_hi, n - KT + 1)
            pe.wait_ge(x1_lo, n - KT + 1)
        for kt in range(KT):
            col = slice(f * P, (f + 1) * P)
            mm = three(pe, ps[:, f, :], mt_hi[:, kt, col], mt_lo[:, kt, col],
                       x_hi[:, kt, chunk], x_lo[:, kt, chunk], kt == 0, kt == KT - 1)
        mm.then_inc(x1_ready, 1)

    def pe_x1_turn(pe, n):
        f = n % KT
        pe.wait_ge(x1_copied, n + 1)
        if real(n - 1):
            pe.wait_ge(x1_added, n - 1)
        else:
            pe.wait_ge(xlo_done, TT)
        for s in range(SUB):
            mm = nc.tensor.transpose(ps[:, 4 + f % 2, s * P:(s + 1) * P],
                                     x1f[:, f % 2, s * P:(s + 1) * P], eye[:])
        mm.then_inc(x1_turned, 1)

    def act_x1(act, n):
        f = n % KT
        act.wait_ge(x1_ready, n + 1)
        if real(n - 1):
            act.wait_ge(x1_turned, n - 1)
        nc.scalar.copy(x1f[:, f % 2], ps[:, f]).then_inc(x1_copied, 1)

    def act_x1_hi(act, c):
        for f in range(KT):
            act.wait_ge(x1_ready, KT * (c + 1))
            nc.scalar.copy(x_hi[:, f, c * CH:(c + 1) * CH], ps[:, f]).then_inc(x1_hi, 1)

    def dve_x1_lo(dve, c):
        chunk = slice(c * CH, (c + 1) * CH)
        for f in range(KT):
            dve.wait_ge(x1_hi, KT * c + f + 1)
            nc.vector.tensor_tensor(x_lo[:, f, chunk], ps[:, f], x_hi[:, f, chunk].bitcast(F32),
                                    ALU.subtract).then_inc(x1_lo, 1)

    def dve_x1_add(dve, n):
        c, f = divmod(n, KT)
        dve.wait_ge(x1_turned, n + 1)
        part = acc[:, SUB * c:SUB * (c + 1), f * P:(f + 1) * P]
        nc.vector.tensor_tensor(part, part, ps[:, 4 + f % 2].rearrange("p (s n) -> p s n", s=SUB),
                                ALU.add).then_inc(x1_added, 1)

    def pe_gate_up(pe, g, gp, c, i, w):
        S = 4 * g + c
        chunk = slice(c * CH, (c + 1) * CH)
        if real(2 * S + (i - 1)):
            pe.wait_ge(silu_done if w == 0 else hmul_done, 2 * S + (i - 1))
        if c == 0:
            pe.wait_ge(lo_done, PER * g + (3 * i + w + 1))
        if isinstance(S, int) and S == 0:
            pe.wait_ge(x1_lo, KT * NCH)
        for kt in range(KT):
            col = slice(kt * P, (kt + 1) * P)
            mm = three(pe, ps[:, 2 * i + w, :], w_hi[gp][:, 3 * i + w, col],
                       w_lo[gp][:, 3 * i + w, col], x_hi[:, kt, chunk],
                       x_lo[:, kt, chunk], kt == 0, kt == KT - 1)
        mm.then_inc(gu, 1)

    def pe_down(pe, g, gp, c, s):
        S = 4 * g + c
        pe.wait_ge(hlo_done, 2 * S + 2)
        if c == 0:
            pe.wait_ge(lo_done, PER * g + PER)
        if real(4 * S + (s - 1)):
            pe.wait_ge(added, 4 * S + (s - 1))
        if isinstance(S, int) and S == 0:
            pe.wait_ge(x1_added, KT * NCH)
        tok = slice(s * P, (s + 1) * P)
        for i in range(2):
            mm = three(pe, ps[:, 4 + s % 2, :], h_hi[:, c % 2, i, tok], h_lo[:, c % 2, i, tok],
                       w_hi[gp][:, 3 * i + 2], w_lo[gp][:, 3 * i + 2], i == 0, i == 1)
        mm.then_inc(down, 1)

    def act_silu(act, g, c, i):
        S = 4 * g + c
        act.wait_ge(gu, 4 * S + (2 * i + 1))
        if real(2 * S + (i - 1)):
            act.wait_ge(hlo_done, 2 * S + (i - 1))
        nc.scalar.activation(hf[:, i], ps[:, 2 * i], ACT.Silu).then_inc(silu_done, 1)

    def dve_hmul(dve, g, c, i):
        S = 4 * g + c
        dve.wait_ge(silu_done, 2 * S + (i + 1))
        dve.wait_ge(gu, 4 * S + (2 * i + 2))
        nc.vector.tensor_tensor(hf[:, i], hf[:, i], ps[:, 2 * i + 1], ALU.mult).then_inc(hmul_done, 1)

    def act_hhi(act, g, c, i):
        S = 4 * g + c
        act.wait_ge(hmul_done, 2 * S + (i + 1))
        if real(4 * (S - 1)):
            act.wait_ge(down, 4 * (S - 1))
        nc.scalar.copy(h_hi[:, c % 2, i], hf[:, i]).then_inc(hhi_done, 1)

    def pool_hlo(pool, g, c, i):
        S = 4 * g + c
        pool.wait_ge(hhi_done, 2 * S + (i + 1))
        nc.gpsimd.tensor_tensor(h_lo[:, c % 2, i], hf[:, i], h_hi[:, c % 2, i].bitcast(F32),
                                ALU.subtract).then_inc(hlo_done, 1)

    def dve_add(dve, g, c, s):
        S = 4 * g + c
        dve.wait_ge(down, 4 * S + (s + 1))
        if real(4 * S + (s - SUB + 1)):
            dve.wait_ge(added, 4 * S + (s - SUB + 1))
        tile = acc[:, SUB * c + s]
        nc.vector.tensor_tensor(tile, tile, ps[:, 4 + s % 2], ALU.add).then_inc(added, 1)

    def pairs(e, body):
        first_unit = lambda g: (ATT + PER) // 2 + PER // 2 * g
        body(0, 0, first_unit(0), 2)
        with e.Fori(0, 2) as it:
            body(it * 2 + 1, 1, it * PER + first_unit(1), 2)
            body(it * 2 + 2, 0, it * PER + first_unit(2), 2)
        body(NG - 2, 1, first_unit(NG - 2), 1)
        body(NG - 1, 0, first_unit(NG - 1), 0)

    def before(g, gp, c):
        return (g, gp, c - 1) if c > 0 else (g - 1, 1 - gp, NCH - 1)

    def started_already(g, c):
        return not (isinstance(g, int) and g == 0 and c == 0)

    def unit(m, k):
        return m + k // 2, k % 2

    def place_of(g, gp, k):
        return (g, gp, k) if k >= 0 else (g - 1, 1 - gp, k + PER)

    const_in, prio_set = sem("const_in"), sem("prio_set")
    ctx_in_s = [sem(f"ctx_in{k}") for k in range(2)]
    out_s = [sem(f"out{k}") for k in range(2)]
    ln = {2: sem("ln2"), 3: sem("ln3")}
    powed = {2: sem("pow2"), 3: sem("pow3")}
    xq_done, xh3_done = sem("xq_done"), sem("xh3_done")
    fwd, evac = sem("fwd"), sem("evac")
    prod, corr_ready = sem("prod"), sem("corr_ready")
    top_done, less_done, topd_done = sem("top_done"), sem("less_done"), sem("topd_done")
    marked, exp_done, summed, divided = sem("marked"), sem("exp_done"), sem("summed"), sem("divided")
    weighed, lag_turned, lag_copied = sem("weighed"), sem("lag_turned"), sem("lag_copied")
    wspec, wneg_copied = sem("wspec"), sem("wneg_copied")
    pcyc, pneg, gathered, x3_done = sem("pcyc"), sem("pneg"), sem("gathered"), sem("x3_done")
    h_turned, h_copied, routed_in = sem("h_turned"), sem("h_copied"), sem("routed_in")
    route, wh_done = sem("route"), sem("wh_done")
    wh_turned, wh_copied, expert, fin_done = (sem("wh_turned"), sem("wh_copied"), sem("expert"),
                                              sem("fin_done"))
    SMALL = 6
    tile_of = lambda big, t: (big[:, t] if isinstance(t, int) else
                              big[:, bass.ds(t, 1)].rearrange("p o d -> p (o d)"))

    def dve_stats(dve, k, src, t, b):
        st_, mv_, ve_ = lst[k][:3]
        n = SMALL * t
        if k == 2:
            by_themselves(dve, t - 1)
            if isinstance(t, int) and t == 0:
                dve.wait_ge(lo_done, PER * NG)
            if real(t - 1):
                dve.wait_ge(xq_done, t - 1)
        else:
            by_themselves(dve, t + 1, t - 1)
            dve.wait_ge(x3_done, t + 1)
            if real(t - 1):
                dve.wait_ge(xh3_done, t - 1)
        nc.vector.bn_stats(st_[:, b], src).then_inc(ln[k], 1)
        by_themselves(dve, n + 1)
        dve.wait_ge(ln[k], n + 1)
        nc.vector.bn_aggr(mv_[:, b], st_[:, b]).then_inc(ln[k], 1)
        dve.wait_ge(ln[k], n + 2)
        nc.vector.tensor_scalar(ve_[:, b:b + 1], mv_[:, b, 1:2], EPS, None, ALU.add).then_inc(ln[k], 1)

    def pool_pow(pool, k, t, b):
        pool.wait_ge(ln[k], SMALL * t + 3)
        nc.gpsimd.tensor_tensor(lst[k][3][:, b:b + 1], lst[k][2][:, b:b + 1], half[:, 0:1],
                                ALU.pow).then_inc(powed[k], 1)

    def dve_normalise(dve, k, src, dst, t, b):
        _, mv_, ve_, pw_, na_, nb_, rs_ = lst[k]
        col = slice(b, b + 1)
        n = SMALL * t
        dve.wait_ge(powed[k], t + 1)
        newton(dve, ln[k], n + 3, ve_[:, col], pw_[:, col], na_[:, col], nb_[:, col], rs_[:, col])
        dve.wait_ge(ln[k], n + 6)
        if k == 2:
            if real(RING * (t - 2) + 1):
                dve.wait_ge(fwd, RING * (t - 2) + 1)
        elif real(t - 1):
            dve.wait_ge(h_turned, t - 1)
        nc.vector.tensor_scalar(dst, src, mv_[:, b, 0:1], rs_[:, col], ALU.subtract,
                                ALU.mult).then_inc(xq_done if k == 2 else xh3_done, 1)

    def sp_ctx(sp, t, b):
        if real(RING * (t - 1) - 1):
            sp.wait_ge(fwd, RING * (t - 1) - 1)
        sp.dma_start(ctx[:, b], row_of(ctx_in, t)).then_inc(ctx_in_s[b], 16)

    TRANSFORMS = [SPEC, KRE, KIM, NRE, NIM]
    RING = len(TRANSFORMS) + 1

    def pe_forward(pe, t, b, h, some):
        for k in some:
            mat = TRANSFORMS[k]
            if k == 0:
                pe.wait_ge(const_in, 48)
                pe.wait_ge(xq_done, t + 1)
                if isinstance(t, int) and t == 0:
                    pe.wait_ge(folded, PER * NG)
            if k == 1:
                pe.wait_ge(ctx_in_s[b], 16 * h + 16)
            if real(RING * t + (k - 1)):
                pe.wait_ge(evac, RING * t + (k - 1))
            nc.tensor.matmul(ps[:, FWD + k % 2], spec[:, mat], (xq if k == 0 else ctx)[:, b],
                             start=True, stop=True).then_inc(fwd, 1)

    def pe_inverse(pe, t, b):
        pe.wait_ge(prod, 2 * t + 2)
        pe.wait_ge(evac, RING * t + (RING - 2))
        nc.tensor.matmul(ps[:, FWD + 1], spec[:, INV_A], p1[:, b], start=True, stop=False)
        nc.tensor.matmul(ps[:, FWD + 1], spec[:, INV_B], p2[:, b], start=False,
                         stop=True).then_inc(fwd, 1)

    def act_evac(act, t, b, some):
        for k in some:
            dst, free, n = ((qs, prod, 2 * (t - 1)), (kre, pcyc, 2 * t - 3), (kim, pcyc, 2 * t - 2),
                            (nre, pneg, 2 * t - 3), (nim, pneg, 2 * t - 2),
                            (ct, corr_ready, t - 1))[k]
            act.wait_ge(fwd, RING * t + (k + 1))
            if real(n):
                act.wait_ge(free, n)
            nc.scalar.copy(dst[:, b], ps[:, FWD + k % 2]).then_inc(evac, 1)

    def dve_products(dve, t, b, some):
        for k in some:
            ctx_part, dst = ((kre, p1), (kim, p2))[k]
            dve.wait_ge(evac, RING * t + (k + 2))
            if real(RING * (t - 1)):
                dve.wait_ge(fwd, RING * (t - 1))
            nc.vector.tensor_tensor(dst[:, b], qs[:, b], ctx_part[:, b], ALU.mult).then_inc(prod, 1)

    def pe_corr(pe, t, b):
        pe.wait_ge(evac, RING * (t + 1))
        if real(t):
            pe.wait_ge(marked, t)
            pe.wait_ge(less_done, t)
        else:
            pe.wait_ge(hmul_done, 2 * NG * NCH - 1)
        for j in range(KT):
            ch = slice(j * P, (j + 1) * P)
            mm = nc.tensor.transpose(ps[:, CORR, ch], ct[:, b, ch], eye[:])
        mm.then_inc(corr_ready, 1)

    def rows(x, b):
        return x[:, b].rearrange("p (r l) -> p r l", l=L)

    def dve_top(dve, t, b):
        corr = ps[:, CORR].rearrange("p (r l) -> p r l", l=L)
        by_themselves(dve, t + 1, 2 * (t - 1))
        dve.wait_ge(corr_ready, t + 1)
        if real(2 * (t - 1)):
            dve.wait_ge(exp_done, 2 * (t - 1))
        for r in range(8):
            mm = nc.vector.max(top[:, b, r], corr[:, r])
        mm.then_inc(top_done, 1)
        largest = top[:, b, :, 0:1]
        dve.wait_ge(top_done, t + 1)
        nc.vector.tensor_tensor(topd[:, b], top[:, b], largest.to_broadcast([P, 8, TOPK]),
                                ALU.subtract).then_inc(topd_done, 1)
        nc.vector.tensor_tensor(rows(cd, b), corr, largest.to_broadcast([P, 8, L]),
                                ALU.subtract).then_inc(less_done, 1)

    def dve_mark(dve, t, b):
        corr = ps[:, CORR].rearrange("p (r l) -> p r l", l=L)
        by_themselves(dve, t - 1)
        if real(t - 1):
            dve.wait_ge(weighed, t - 1)
        for r in range(8):
            mm = nc.vector.match_replace(rows(mark, b)[:, r], top[:, b, r], corr[:, r], MARK)
        mm.then_inc(marked, 1)

    def act_exp(act, t, b):
        act.wait_ge(topd_done, t + 1)
        flat = topd[:, b].rearrange("p r k -> p (r k)")
        nc.scalar.activation(flat, flat, ACT.Exp).then_inc(exp_done, 1)
        act.wait_ge(less_done, t + 1)
        if real(t - 1):
            act.wait_ge(divided, t - 1)
        nc.scalar.activation(ex[:, b], cd[:, b], ACT.Exp).then_inc(exp_done, 1)

    def dve_sum(dve, t, b):
        dve.wait_ge(exp_done, 2 * t + 1)
        if real(t - 1):
            dve.wait_ge(divided, t - 1)
        nc.vector.tensor_reduce(zs[:, b], topd[:, b], AX.X, ALU.add).then_inc(summed, 1)
        dve.wait_ge(summed, 2 * t + 1)
        nc.vector.reciprocal(rz[:, b], zs[:, b]).then_inc(summed, 1)

    def pool_divide(pool, t, b):
        pool.wait_ge(exp_done, 2 * t + 2)
        pool.wait_ge(summed, 2 * t + 2)
        if real(t - 1):
            pool.wait_ge(weighed, t - 1)
        nc.gpsimd.tensor_tensor(rows(en, b), rows(ex, b), rz[:, b].unsqueeze(2).to_broadcast([P, 8, L]),
                                ALU.mult).then_inc(divided, 1)

    def dve_weigh(dve, t, b):
        dve.wait_ge(divided, t + 1)
        dve.wait_ge(marked, t + 1)
        if real(t - 1):
            dve.wait_ge(lag_turned, t - 1)
        nc.vector.scalar_tensor_tensor(out=wl[:, b], in0=mark[:, b], scalar=MARK, in1=en[:, b],
                                       op0=ALU.is_equal, op1=ALU.mult).then_inc(weighed, 1)

    def pe_lags(pe, t, b):
        pe.wait_ge(weighed, t + 1)
        if isinstance(t, int) and t == 0:
            pe.wait_ge(added, 4 * NCH * NG)
        if real(t):
            pe.wait_ge(x3_done, t)
        for j in range(KT):
            ch = slice(j * P, (j + 1) * P)
            mm = nc.tensor.transpose(ps[:, LAGS, ch], wl[:, b, ch], eye[:])
        mm.then_inc(lag_turned, 1)

    def pe_cyclic(pe, t, b):
        pe.wait_ge(lag_copied, t + 1)
        if real(2 * t):
            pe.wait_ge(pcyc, 2 * t)
        nc.tensor.matmul(ps[:, WCYC], spec[:, SPEC], wts[:, b], start=True, stop=True).then_inc(wspec, 1)

    def pe_negacyclic(pe, t, b):
        if real(t):
            pe.wait_ge(wneg_copied, t)
        nc.tensor.matmul(ps[:, WNEG], spec[:, NEG], wts[:, b], start=True, stop=True).then_inc(wspec, 1)

    def act_lags(act, t, b):
        act.wait_ge(lag_turned, t + 1)
        if real(2 * (t - 1)):
            act.wait_ge(wspec, 2 * (t - 1))
        nc.scalar.copy(wts[:, b], ps[:, LAGS]).then_inc(lag_copied, 1)

    def act_negacyclic(act, t, b):
        act.wait_ge(wspec, 2 * t + 2)
        if real(2 * (t - 1)):
            act.wait_ge(pneg, 2 * (t - 1))
        nc.scalar.copy(wns[:, b], ps[:, WNEG]).then_inc(wneg_copied, 1)

    def dve_cyclic(dve, t, b):
        dve.wait_ge(wspec, 2 * t + 1)
        if real(t - 1):
            dve.wait_ge(gathered, t - 1)
        nc.vector.tensor_tensor(pc1[:, b], ps[:, WCYC], kre[:, b], ALU.mult).then_inc(pcyc, 1)
        nc.vector.tensor_tensor(pc2[:, b], ps[:, WCYC], kim[:, b], ALU.mult).then_inc(pcyc, 1)

    def pool_negacyclic(pool, t, b):
        pool.wait_ge(wneg_copied, t + 1)
        if real(t - 1):
            pool.wait_ge(gathered, t - 1)
        nc.gpsimd.tensor_tensor(pn1[:, b], wns[:, b], nre[:, b], ALU.mult).then_inc(pneg, 1)
        nc.gpsimd.tensor_tensor(pn2[:, b], wns[:, b], nim[:, b], ALU.mult).then_inc(pneg, 1)

    def pe_gather(pe, t, b, parts):
        for k in parts:
            mat, src, ready = ((OUT_A, pc1, pcyc), (OUT_B, pc2, pcyc), (OUT_NA, pn1, pneg),
                               (OUT_NB, pn2, pneg))[k]
            if k == 0:
                pe.wait_ge(lag_copied, t + 1)
            pe.wait_ge(ready, 2 * t + (k % 2 + 1))
            mm = nc.tensor.matmul(ps[:, LAGS], spec[:, mat], src[:, b], start=(k == 0), stop=(k == 3))
            if k == 3:
                mm.then_inc(gathered, 1)

    def dve_x3(dve, t, b):
        dve.wait_ge(gathered, t + 1)
        if real(t - 1):
            dve.wait_ge(fin_done, t - 1)
        nc.vector.tensor_tensor(x3[:, b], tile_of(acc, t), ps[:, LAGS], ALU.add).then_inc(x3_done, 1)

    def pe_turn_h(pe, t, b):
        pe.wait_ge(xh3_done, t + 1)
        if real(t):
            pe.wait_ge(fin_done, t)
        for j in range(KT):
            ch = slice(j * P, (j + 1) * P)
            mm = nc.tensor.transpose(ps[:, MISC, ch], xh3[:, b, ch], eye[:])
        mm.then_inc(h_turned, 1)

    def act_turn_h(act, t, b):
        act.wait_ge(h_turned, t + 1)
        if real(t - 1):
            act.wait_ge(routed_in, t - 1)
        nc.scalar.copy(x3t[:, b], ps[:, MISC]).then_inc(h_copied, 1)

    def pe_route(pe, t, b):
        pe.wait_ge(h_copied, t + 1)
        if real(t):
            pe.wait_ge(wh_copied, t)
        for j in range(KT):
            mm = nc.tensor.matmul(ps[:, ROUTE, 0:P + E], x3t[:, b, j * P:(j + 1) * P], rt[:, j],
                                  start=(j == 0), stop=(j == KT - 1))
        mm.then_inc(routed_in, 1)

    def dve_route(dve, t, b):
        logits = ps[:, ROUTE, P:P + E]
        n = 4 * t
        by_themselves(dve, t + 1, 4 * (t - 1))
        dve.wait_ge(routed_in, t + 1)
        if real(4 * (t - 1)):
            dve.wait_ge(route, 4 * (t - 1))
        nc.vector.max(mx[:, b], logits).then_inc(route, 1)
        dve.wait_ge(route, n + 1)
        dve.wait_ge(prio_set, E)
        nc.vector.scalar_tensor_tensor(out=sc[:, b], in0=logits, scalar=mx[:, b, 0:1], in1=prio[:],
                                       op0=ALU.is_equal, op1=ALU.mult).then_inc(route, 1)
        by_themselves(dve, n + 2)
        dve.wait_ge(route, n + 2)
        nc.vector.max(m2[:, b], sc[:, b]).then_inc(route, 1)
        dve.wait_ge(route, n + 3)
        nc.vector.tensor_scalar(rw[:, b], sc[:, b], m2[:, b, 0:1], mx[:, b, 0:1], ALU.is_equal,
                                ALU.mult).then_inc(route, 1)
        dve.wait_ge(route, n + 4)
        if real(t - 1):
            dve.wait_ge(wh_turned, t - 1)
        nc.vector.tensor_tensor(wh[:, b].rearrange("p (e r) -> p e r", e=E),
                                ps[:, ROUTE, 0:P].rearrange("p (e r) -> p e r", e=E),
                                rw[:, b].unsqueeze(2).to_broadcast([P, E, R]),
                                ALU.mult).then_inc(wh_done, 1)

    def pe_turn_wh(pe, t, b):
        pe.wait_ge(wh_done, t + 1)
        nc.tensor.transpose(ps[:, ROUTE, 2 * P:3 * P], wh[:, b], eye[:]).then_inc(wh_turned, 1)

    def pe_expert(pe, t, b):
        pe.wait_ge(wh_copied, t + 1)
        pe.wait_ge(h_copied, t + 1)
        nc.tensor.matmul(ps[:, MISC], wht[:, b], eb[:], start=True, stop=True).then_inc(expert, 1)

    def act_expert(act, t, b):
        act.wait_ge(wh_turned, t + 1)
        if real(t - 1):
            act.wait_ge(expert, t - 1)
        nc.scalar.copy(wht[:, b], ps[:, ROUTE, 2 * P:3 * P]).then_inc(wh_copied, 1)

    def dve_final(dve, t, b, h):
        dve.wait_ge(expert, t + 1)
        if not isinstance(t, int) or t >= 2:
            dve.wait_ge(out_s[b], 16 * h)
        nc.vector.tensor_tensor(fin[:, b], x3[:, b], ps[:, MISC], ALU.add).then_inc(fin_done, 1)

    def sp_store(sp, t, b):
        sp.wait_ge(fin_done, t + 1)
        sp.dma_start(row_of(out, t), fin[:, b]).then_inc(out_s[b], 16)

    DEEP = 3

    PEEL = 6

    def slots(e, piece, first=1):
        def slot(v, par, hv):
            def at(stage):
                b = (par - stage) % 2
                h = hv + (par - stage - b) // 2
                t = 2 * h + b
                return None if isinstance(t, int) and not 0 <= t < TT else (t, b, h)
            piece(at)
        for v in range(first, PEEL):
            slot(v, v % 2, v // 2)
        with e.Fori(0, (TT - PEEL) // 2 - 1) as it:
            for k in range(2):
                slot(None, k, it + PEEL // 2)
        for v in range(TT - 2, TT + DEEP):
            slot(v, v % 2, v // 2)

    LEAD = ATT + PER
    PRE = ATT + 1
    X1_HALVES = [0, 1, 2, 4, 5, 6, 8, 9, 10]

    with nc.Block() as block:

        @block.sync
        def _(sp):
            sp_unit(sp, 0, 0)
            sp_unit(sp, 0, 1)
            sp.dma_start(nat_scale[:], scale_nat).then_inc(nat_in, 16)
            sp.dma_start(eye[:], eye_in).then_inc(eye_in_s, 16)
            def x_load(c):
                src = x[SUB * c:SUB * (c + 1)].rearrange("s p d -> p s d")
                sp.dma_start(acc[:, SUB * c:SUB * (c + 1)], src).then_inc(x_in[c], 16)
            x_load(0)
            sp.wait_ge(zeroed, 4)
            sp.dma_start(lattn[0:3 * R, 0:2, :], lora_attn[0]).then_inc(lora_in, 16)
            sp.dma_start(lattn[0:R, 2:4, :], lora_attn[1][0:R]).then_inc(lora_in, 16)
            sp.dma_start(lh[0:KT * R], lora_h).then_inc(lora_in, 16)
            sp.dma_start(ldown[0:R], lora_down_b).then_inc(lora_in, 16)
            for b in range(2):
                lft_parts(sp, lora_ft[b], b)
            for c in range(1, NCH):
                x_load(c)
            for v in range(2, LEAD):
                sp_unit(sp, v // 2, v % 2, rows=v < KT or v >= ATT)

            def body(g, gp, m, ahead):
                if ahead:
                    for k in range(PER):
                        if k % 3 == 0:
                            lft_load(sp, g * 2 + (2 + k // 3), k // 3)
                        sp_unit(sp, *unit(m, k))
            pairs(sp, body)
            sp.wait_ge(lo_done, PER * NG)
            for dst, src in ((spec, spectral), (rt, router), (eb, expert_b)):
                sp.dma_start(dst[:], src).then_inc(const_in, 16)

            def piece(at):
                if a := at(0):
                    sp_ctx(sp, a[0], a[1])
                if a := at(3):
                    sp_store(sp, a[0], a[1])
            slots(sp, piece, 0)
            for b in range(2):
                sp.wait_ge(out_s[b], 16 * TT // 2)

        @block.gpsimd
        def _(pool):
            for k, buf in enumerate((lattn, lh, lft, ldown)):
                nc.gpsimd.memset(buf[:], 0.0).then_inc(zeroed, 1)
            nc.gpsimd.memset(half[:], -0.5).then_inc(started, 1)
            pool.wait_ge(started, 1)
            pool_centre(pool, 0, 0)
            for v in range(LEAD + 1):
                if v < LEAD:
                    pool_last(pool, v // 2, v % 2)
                    pool_centre(pool, (v + 1) // 2, (v + 1) % 2)
                if v >= 1:
                    nat = v - 1 - KT if KT <= v - 1 < ATT else None
                    pool_scale(pool, (v - 1) // 2, (v - 1) % 2, nat)
                if 1 <= v <= ATT:
                    pool_fold(pool, v - 1)
                if v - 2 >= ATT:
                    pool_lo(pool, (v - 2) // 2, v % 2, 0, v - 2 - ATT)
                if v % SUB == 0 and v // SUB < NCH:
                    x_pow(pool, v // SUB)

            def body(g, gp, m, ahead):
                for c in range(NCH):
                    k = 3 * (c // 2)
                    if ahead and c % 2 == 0:
                        pool_last(pool, *unit(m, k))
                        pool_centre(pool, *unit(m, k + 1))
                        _, wp, wk = place_of(g + 1, 1 - gp, k - 1)
                        pool_lo(pool, *unit(m, k - 1), wp, wk)
                        pool_scale(pool, *unit(m, k))
                        pool_hlo(pool, g, c, 0)
                        pool_last(pool, *unit(m, k + 1))
                        pool_centre(pool, *unit(m, k + 2))
                        pool_lo(pool, *unit(m, k), 1 - gp, k)
                        pool_hlo(pool, g, c, 1)
                    elif ahead:
                        pool_scale(pool, *unit(m, k + 1))
                        pool_last(pool, *unit(m, k + 2))
                        if ahead == 2 or c == 1:
                            pool_centre(pool, *unit(m, k + 3))
                        pool_lo(pool, *unit(m, k + 1), 1 - gp, k + 1)
                        pool_hlo(pool, g, c, 0)
                        pool_scale(pool, *unit(m, k + 2))
                        pool_hlo(pool, g, c, 1)
                    else:
                        if c == 0:
                            pool_lo(pool, *unit(m, -1), gp, PER - 1)
                        if c == 2:
                            pool_pow(pool, 2, 0, 0)
                            pool_pow(pool, 2, 1, 1)
                        pool_hlo(pool, g, c, 0)
                        pool_hlo(pool, g, c, 1)
            pairs(pool, body)
            for k in range(E):
                nc.gpsimd.memset(prio[:, k:k + 1], float(E - k)).then_inc(prio_set, 1)

            pool_divide(pool, 0, 0)

            def piece(at):
                if a := at(2):
                    pool_pow(pool, 3, *a[:2])
                if a := at(1):
                    pool_negacyclic(pool, *a[:2])
                if a := at(-1):
                    pool_pow(pool, 2, *a[:2])
                if a := at(0):
                    pool_divide(pool, *a[:2])
            slots(pool, piece)

        @block.scalar
        def _(act):
            act_lines(act, 0, 0, EARLY)

            def slot(v):
                act_lines(act, v // 2, v % 2, LATE)

            def slot_on(v):
                act_lines(act, (v + 1) // 2, (v + 1) % 2, EARLY)
                if v - 1 >= ATT:
                    act_hi(act, (v - 1) // 2, (v - 1) % 2, 0, 0, v - 1 - ATT)
            for v in range(PRE):
                if v >= 2:
                    x_hi_copy(act, v - 2)
                slot(v)
                slot_on(v)
                if v < KT:
                    for k in (2 * v, 2 * v + 1):
                        act.wait_ge(al_ready, k + 1)
                        dst = w3[:, k] if k < KT else wsum[:, k - KT]
                        nc.scalar.copy(dst, ps[:, k % KT]).then_inc(al_copied, 1)
                if v >= 1:
                    x_normalise(act, v - 1)
            x_hi_copy(act, TT - 1)
            slot(PRE)
            act_mt(act)
            for n in range(KT * NCH):
                if n in X1_HALVES:
                    j = X1_HALVES.index(n)
                    (slot if j % 2 else slot_on)(PRE + (j + 1) // 2)
                act_x1(act, n)
                if n % KT == KT - 1:
                    act_x1_hi(act, n // KT)

            def body(g, gp, m, ahead):
                for c in range(NCH):
                    k = 3 * (c // 2)
                    if ahead and c % 2 == 0:
                        act_lines(act, *unit(m, k), LATE)
                        act_silu(act, g, c, 0)
                        act_lines(act, *unit(m, k + 1), EARLY)
                        wg, wp, wk = place_of(g + 1, 1 - gp, k - 1)
                        act_hi(act, *unit(m, k - 1), wp, wg, wk)
                        act_hhi(act, g, c, 0)
                        act_lines(act, *unit(m, k + 1), LATE)
                        act_silu(act, g, c, 1)
                        act_hi(act, *unit(m, k), 1 - gp, g + 1, k)
                        act_hhi(act, g, c, 1)
                    elif ahead:
                        act_lines(act, *unit(m, k + 2), EARLY)
                        act_silu(act, g, c, 0)
                        act_lines(act, *unit(m, k + 2), LATE)
                        act_hi(act, *unit(m, k + 1), 1 - gp, g + 1, k + 1)
                        act_hhi(act, g, c, 0)
                        if ahead == 2 or c == 1:
                            act_lines(act, *unit(m, k + 3), EARLY)
                        act_silu(act, g, c, 1)
                        act_hhi(act, g, c, 1)
                    else:
                        if c == 0:
                            act_hi(act, *unit(m, -1), gp, g, PER - 1)
                        act_silu(act, g, c, 0)
                        act_hhi(act, g, c, 0)
                        act_silu(act, g, c, 1)
                        act_hhi(act, g, c, 1)
                        if c == 2:
                            act_evac(act, 0, 0, range(RING))
            pairs(act, body)
            act_exp(act, 0, 0)
            act.wait_ge(added, 4 * NCH * NG)

            def piece(at):
                if a := at(0):
                    act_evac(act, *a[:2], (0, 1))
                if a := at(1):
                    act_lags(act, *a[:2])
                if a := at(0):
                    act_evac(act, *a[:2], (2,))
                if a := at(1):
                    act_negacyclic(act, *a[:2])
                if a := at(0):
                    act_evac(act, *a[:2], (3, 4, 5))
                if a := at(2):
                    act_turn_h(act, *a[:2])
                if a := at(0):
                    act_exp(act, *a[:2])
                if a := at(2):
                    act_expert(act, *a[:2])
            slots(act, piece)

        @block.vector
        def _(dve):
            dve.wait_ge(started, 1)
            dve.wait_ge(eye_in_s, 16)
            nc.vector.tensor_scalar(eye3[:], eye[:], 3.0, None, ALU.mult).then_inc(eye3_made, 1)

            def slot(v):
                dve_mix(dve, v // 2, v % 2)

            def slot_on(v):
                if v - 1 >= ATT:
                    dve_fold(dve, (v - 1) // 2, (v - 1) % 2)
                dve_mix_on(dve, v // 2, v % 2)
            for v in range(PRE):
                if v >= 3:
                    x_lo_sub(dve, v - 3)
                slot(v)
                if v % SUB == 1:
                    x_rstd(dve, v // SUB)
                slot_on(v)
                if v % SUB == 0 and v < TT:
                    x_stats(dve, v // SUB)
            x_lo_sub(dve, TT - 2)
            x_lo_sub(dve, TT - 1)
            slot(PRE)
            dve_mt(dve)
            for n in range(KT * NCH):
                if n in X1_HALVES:
                    j = X1_HALVES.index(n)
                    (slot if j % 2 else slot_on)(PRE + (j + 1) // 2)
                if n % KT == KT - 1:
                    dve_x1_lo(dve, n // KT)
                if n > 0:
                    dve_x1_add(dve, n - 1)
            dve_x1_add(dve, KT * NCH - 1)

            def body(g, gp, m, ahead):
                for c in range(NCH):
                    k = 3 * (c // 2)
                    last = before(g, gp, c)[0::2]
                    if ahead and c % 2 == 0:
                        dve_mix(dve, *unit(m, k))
                        dve_fold(dve, *unit(m, k - 1))
                        dve_mix_on(dve, *unit(m, k))
                    elif ahead:
                        dve_mix_on(dve, *unit(m, k + 1))
                        dve_mix(dve, *unit(m, k + 2))
                        dve_fold(dve, *unit(m, k + 1))
                    elif c == 0:
                        dve_fold(dve, *unit(m, -1))
                    dve_hmul(dve, g, c, 0)
                    if started_already(g, c):
                        dve_add(dve, *last, 0)
                        dve_add(dve, *last, 1)
                    if ahead and c % 2 == 0:
                        dve_mix(dve, *unit(m, k + 1))
                        dve_fold(dve, *unit(m, k))
                    elif ahead:
                        dve_mix_on(dve, *unit(m, k + 2))
                    if started_already(g, c):
                        dve_add(dve, *last, 2)
                    dve_hmul(dve, g, c, 1)
                    if started_already(g, c):
                        dve_add(dve, *last, 3)
                    if not ahead and c == 1:
                        for t in range(2):
                            dve_stats(dve, 2, acc[:, t], t, t)
                            dve_normalise(dve, 2, acc[:, t], xq[:, t], t, t)
                    if not ahead and c == 2:
                        dve_products(dve, 0, 0, (0, 1))
            pairs(dve, body)
            dve_top(dve, 0, 0)
            dve_mark(dve, 0, 0)
            dve_add(dve, NG - 1, NCH - 1, 0)
            dve_add(dve, NG - 1, NCH - 1, 1)
            dve_sum(dve, 0, 0)
            dve_add(dve, NG - 1, NCH - 1, 2)
            dve_add(dve, NG - 1, NCH - 1, 3)
            dve.wait_ge(added, 4 * NCH * NG)

            def piece(at):
                if a := at(1):
                    dve_weigh(dve, *a[:2])
                if a := at(2):
                    dve_stats(dve, 3, x3[:, a[1]], *a[:2])
                if a := at(0):
                    dve_products(dve, *a[:2], (0,))
                if a := at(2):
                    dve_normalise(dve, 3, x3[:, a[1]], xh3[:, a[1]], *a[:2])
                if a := at(0):
                    dve_products(dve, *a[:2], (1,))
                if a := at(1):
                    dve_cyclic(dve, *a[:2])
                if a := at(-1):
                    dve_stats(dve, 2, tile_of(acc, a[0]), *a[:2])
                if a := at(3):
                    dve_final(dve, *a)
                if a := at(-1):
                    dve_normalise(dve, 2, tile_of(acc, a[0]), xq[:, a[1]], *a[:2])
                if a := at(0):
                    dve_top(dve, *a[:2])
                    dve_sum(dve, *a[:2])
                if a := at(2):
                    dve_route(dve, *a[:2])
                if a := at(0):
                    dve_mark(dve, *a[:2])
                if a := at(1):
                    dve_x3(dve, *a[:2])
            slots(dve, piece)

        @block.tensor
        def _(pe):
            pe.wait_ge(zeroed, 4)
            pe.wait_ge(lora_in, 64)
            for k in range(2 * KT):
                if real(k - KT + 1):
                    pe.wait_ge(al_copied, k - KT + 1)
                rows_ = slice((k % KT) * P, (k % KT + 1) * P)
                lhs, rhs = ((lattn[:, 2, rows_], lattn[:, 3]) if k < KT else
                            (lattn[:, 1, rows_], lattn[:, 0]))
                nc.tensor.matmul(ps[:, k % KT], lhs, rhs, start=True, stop=True).then_inc(al_ready, 1)

            def lora(v):
                pe_lora(pe, v // 2, v % 2, 0, v - ATT)
            for v in range(PRE):
                if v >= 1:
                    x_turn(pe, v - 1)
                if v >= ATT:
                    lora(v)
                if v > KT and (v - KT) % 3 == 0:
                    pe_mt(pe, (v - KT) // 3 - 1)
            lora(PRE)
            for n in range(KT * NCH):
                if n in X1_HALVES[1::2]:
                    lora(PRE + (X1_HALVES.index(n) + 1) // 2)
                pe_x1(pe, n)
                if n % KT > 0:
                    pe_x1_turn(pe, n - 1)
                if n % KT == KT - 1:
                    pe_x1_turn(pe, n)

            def body(g, gp, m, ahead):
                for c in range(NCH):
                    k = 3 * (c // 2)
                    last = before(g, gp, c)
                    downs = started_already(g, c)
                    pe_gate_up(pe, g, gp, c, 0, 0)
                    if not ahead and c == 3:
                        pe_forward(pe, 0, 0, 0, range(5))
                    if ahead:
                        pe_lora(pe, *unit(m, k + c % 2), g + 1, k + c % 2)
                    pe_gate_up(pe, g, gp, c, 0, 1)
                    if downs:
                        pe_down(pe, *last, 0)
                        pe_down(pe, *last, 1)
                    if not ahead and c == 3:
                        pe_inverse(pe, 0, 0)
                    pe_gate_up(pe, g, gp, c, 1, 0)
                    if downs:
                        pe_down(pe, *last, 2)
                    if ahead and c % 2 == 1:
                        pe_lora(pe, *unit(m, k + 2), g + 1, k + 2)
                    pe_gate_up(pe, g, gp, c, 1, 1)
                    if not ahead and c == 3:
                        pe_corr(pe, 0, 0)
                    if downs:
                        pe_down(pe, *last, 3)
            pairs(pe, body)
            for s in range(SUB):
                pe_down(pe, NG - 1, 0, NCH - 1, s)

            def piece(at):
                if a := at(0):
                    pe_forward(pe, *a, (0, 1))
                if a := at(1):
                    pe_lags(pe, *a[:2])
                if a := at(3):
                    pe_expert(pe, *a[:2])
                if a := at(0):
                    pe_forward(pe, *a, (2,))
                if a := at(1):
                    pe_cyclic(pe, *a[:2])
                    pe_negacyclic(pe, *a[:2])
                if a := at(0):
                    pe_forward(pe, *a, (3, 4))
                    pe_inverse(pe, *a[:2])
                if a := at(2):
                    pe_turn_h(pe, *a[:2])
                if a := at(0):
                    pe_corr(pe, *a[:2])
                if a := at(1):
                    pe_gather(pe, *a[:2], (0,))
                if a := at(2):
                    pe_route(pe, *a[:2])
                if a := at(1):
                    pe_gather(pe, *a[:2], (1,))
                    pe_gather(pe, *a[:2], (2, 3))
                if a := at(2):
                    pe_turn_wh(pe, *a[:2])
            slots(pe, piece)
    st.close()


def kernel(x, ctx_4096, L0_attn_codes_attn, L0_attn_scales_attn, L0_attn_codes_gu,
           L0_attn_scales_gu, L0_attn_codes_down, L0_attn_scales_down, L0_attn_lora_A_h,
           L0_attn_lora_A_down, L0_attn_lora_B_attn, L0_attn_lora_B_gu, L0_attn_lora_B_down,
           L0_ffn_route_w, L0_ffn_A, L0_ffn_Bw):
    import concourse.bacc as bacc
    from concourse.bass_utils import run_bass_kernel_spmd

    arr = lambda a: np.asarray(a)
    ca, cgu, cd = arr(L0_attn_codes_attn), arr(L0_attn_codes_gu), arr(L0_attn_codes_down)
    sa, sgu, sd = arr(L0_attn_scales_attn), arr(L0_attn_scales_gu), arr(L0_attn_scales_down)
    ah, ad = arr(L0_attn_lora_A_h), arr(L0_attn_lora_A_down)
    ba, bgu, bd = arr(L0_attn_lora_B_attn), arr(L0_attn_lora_B_gu), arr(L0_attn_lora_B_down)
    nat = ca[:3].reshape(3, KT, P, D).transpose(1, 0, 2, 3).reshape(NAT, P, D)
    tr = ca[3].T.reshape(KT, P, D)
    gu = cgu.reshape(2, NFT, P, KT, P).transpose(1, 0, 4, 3, 2).reshape(NFT, 2, P, D)
    dn = cd.T.reshape(NFT, 1, P, D)
    ft = np.concatenate([gu, dn], axis=1).reshape(3 * NFT, P, D)
    codes = np.concatenate([tr, nat, ft])
    scale_nat = sa[:3].reshape(3, KT, P, D // QB).transpose(2, 1, 0, 3).reshape(P, NAT, D // QB)
    s_tr = sa[3].T.reshape(KT, 2, D)
    s_gu = sgu.reshape(2, NFT, P, KT, 2).transpose(1, 0, 4, 3, 2).reshape(NFT, 2, 2, D)
    s_dn = sd.T.reshape(NFT, 1, 2, D)
    s_ft = np.concatenate([s_gu, s_dn], axis=1).reshape(3 * NFT, 2, D)
    scale_rows = np.concatenate([s_tr, s_ft]).reshape(-1, 1, D)
    lora_attn = np.zeros((2, 3 * R, 2, D), np.float32)
    lora_attn[0, :, 0] = ah[:3].reshape(3 * R, D)
    lora_attn[0, :, 1] = ba[:3].transpose(0, 2, 1).reshape(3 * R, D)
    lora_attn[1, :R, 0] = ah[3]
    lora_attn[1, :R, 1] = ba[3].T
    lora_h = ah[4:6].reshape(2, R, KT, P).transpose(2, 1, 0, 3).reshape(KT * R, 2, P)
    b_t = bgu.reshape(2, NFT, P, R).transpose(1, 3, 0, 2).reshape(NFT, R, 2 * P)
    a_t = ad.reshape(R, NFT, P).transpose(1, 0, 2)
    lora_ft = np.concatenate([b_t, a_t], axis=2)
    cols = np.concatenate([arr(L0_ffn_A).reshape(P, D), arr(L0_ffn_route_w)]).T
    router = cols.reshape(KT, P, P + E).transpose(1, 0, 2)
    expert_b = arr(L0_ffn_Bw).transpose(0, 2, 1).reshape(P, D)
    given = {
        "x": arr(x).reshape(TT, P, D), "ctx": arr(ctx_4096).reshape(TT, P, D), "codes": codes,
        "scale_nat": scale_nat, "scale_rows": scale_rows, "lora_attn": lora_attn,
        "lora_h": lora_h, "lora_ft": lora_ft, "lora_down_b": bd.T, "router": router,
        "expert_b": expert_b, "spectral": spectral_matrices(), "eye": np.eye(P, dtype=np.float32),
    }
    given = {f"in_{k}": np.ascontiguousarray(v) for k, v in given.items()}
    nc = bacc.Bacc("TRN2", target_bir_lowering=False, num_devices=1)
    args = [nc.dram_tensor(k, v.shape, mybir.dt.from_np(v.dtype), kind="ExternalInput").ap()
            for k, v in given.items()]
    out = nc.dram_tensor("out", (TT, P, D), F32, kind="ExternalOutput").ap()
    build(nc, *args, out)
    r = run_bass_kernel_spmd(nc, [given], core_ids=[0])
    return r.results[0]["out"].reshape(SEQS, L, D)
```
